# Optimizing a Trainium2 kernel written in Bass

```python
import numpy as np
import jax
import jax.numpy as jnp

def _softmax(x, axis=-1):
    return jax.nn.softmax(x, axis=axis)

def _gelu(x):
    return jax.nn.gelu(x, approximate=True)

def _silu(x):
    return jax.nn.silu(x)

def _sigmoid(x):
    return jax.nn.sigmoid(x)

def _layernorm(x, axis=-1, eps=1e-05):
    m = jnp.mean(x, axis=axis, keepdims=True)
    v = jnp.var(x, axis=axis, keepdims=True)
    return (x - m) / jnp.sqrt(v + eps)

def _scatter_add(tgt, idx, src, axis=0):
    return tgt.at[idx].add(src)

def _segment_sum(src, seg, n):
    return jax.ops.segment_sum(src, seg, n)
kernel_name = 'mk_xattn_seq_d4_seqx_r8_c623bf'

def setup_inputs(seed: int=0):
    np.random.seed(seed)
    _w = jnp.asarray

    def _rec_inputs():
        import jax
        import jax.numpy as jnp
        _rk = jax.random.key(seed)
        x = -0.0002928 + 1 * jax.random.normal(jax.random.fold_in(_rk, 1), (128, 64, 128), jnp.float32)
        _lenS = 64 - jax.random.randint(jax.random.fold_in(_rk, 7), (128,), 0, max(1, 64 // 4) + 1, jnp.int32)
        _lenS2 = 64 - jax.random.randint(jax.random.fold_in(_rk, 8), (128,), 0, max(1, 64 // 4) + 1, jnp.int32)
        _ctx_1024P = jax.random.normal(jax.random.fold_in(_rk, 11), (128, 16, 128), jnp.float32)
        _ctx_1024c = jax.random.dirichlet(jax.random.fold_in(_rk, 511), 0.3 * jnp.ones((16,), jnp.float32), (128, 64))
        _ctx_1024t = jnp.einsum('bsk,bkd->bsd', _ctx_1024c, _ctx_1024P)
        _ctx_1024t = _ctx_1024t * jax.lax.rsqrt(jnp.mean(jnp.square(_ctx_1024t)) + 1e-12) * 0.953939
        ctx_1024 = -1.39393e-06 + 0.999914 * (_ctx_1024t + 0.3 * jax.random.normal(jax.random.fold_in(_rk, 611), (128, 64, 128), jnp.float32))
        _validS = jnp.arange(64)[None, :] < _lenS[:, None]
        _validS2 = jnp.arange(64)[None, :] < _lenS2[:, None]
        _causal = jnp.tril(jnp.ones((64, 64), dtype=bool))
        mask_BxS2_bf1 = jnp.ones((128, 64), dtype=bool)
        return (x, ctx_1024, mask_BxS2_bf1)
    x, ctx_1024, mask_BxS2_bf1 = _rec_inputs()

    def _L0_xattn_setup():
        import jax, jax.numpy as jnp
        import numpy as np
        EPS = 1e-05

        def _layernorm(x, g, b):
            m = jnp.mean(x, axis=-1, keepdims=True)
            v = jnp.mean((x - m) ** 2, axis=-1, keepdims=True)
            return (x - m) / jnp.sqrt(v + EPS) * g + b

        def _mha(x, kv, Wq, Wk, Wv, mask, causal):
            m = mask[:, None]
            Q = jnp.einsum('bsd,hdk->bhsk', x, Wq) * m
            K = jnp.einsum('bsd,hdk->bhsk', kv, Wk) * m
            V = jnp.einsum('bsd,hdk->bhsk', kv, Wv) * m
            energy = jnp.einsum('bhsk,bhtk->bhst', Q, K)
            S = energy.shape[-1]
            lengths = jnp.sum(energy[:, :, 0, :] != 0, axis=-1)
            cols = jnp.arange(S)
            energy = jnp.where(cols[None, None, None, :] >= lengths[:, :, None, None], -jnp.inf, energy)
            if causal:
                energy = jnp.where(cols[None, :] > cols[:, None], -jnp.inf, energy)
            dk = Wq.shape[-1]
            score = jax.nn.softmax(energy / jnp.sqrt(jnp.asarray(dk, energy.dtype)), axis=-1)
            out = jnp.einsum('bhst,bhtk->bhsk', score, V) * m
            B, H, Sx, dkk = out.shape
            return out.transpose(0, 2, 1, 3).reshape(B, Sx, H * dkk)
        key = jax.random.key(seed)
        ks = jax.random.split(key, 20)
        B, S, D, H = (2, 256, 128, 16)
        dk = D // H
        sd = 0.02
        inp = {'x': jax.random.normal(ks[0], (B, S, D), jnp.float32), 'context': jax.random.normal(ks[1], (B, S, D), jnp.float32), 'Wq1': jax.random.normal(ks[2], (H, D, dk), jnp.float32) * sd, 'Wk1': jax.random.normal(ks[3], (H, D, dk), jnp.float32) * sd, 'Wv1': jax.random.normal(ks[4], (H, D, dk), jnp.float32) * sd, 'Wq2': jax.random.normal(ks[5], (H, D, dk), jnp.float32) * sd, 'Wk2': jax.random.normal(ks[6], (H, D, dk), jnp.float32) * sd, 'Wv2': jax.random.normal(ks[7], (H, D, dk), jnp.float32) * sd, 'ln1_g': jnp.ones((D,), jnp.float32), 'ln1_b': jnp.zeros((D,), jnp.float32), 'ln2_g': jnp.ones((D,), jnp.float32), 'ln2_b': jnp.zeros((D,), jnp.float32), 'ln3_g': jnp.ones((D,), jnp.float32), 'ln3_b': jnp.zeros((D,), jnp.float32), 'fc1_w': jax.random.normal(ks[8], (D, D), jnp.float32) * sd, 'fc1_b': jnp.zeros((D,), jnp.float32), 'fc2_w': jax.random.normal(ks[9], (D, D), jnp.float32) * sd, 'fc2_b': jnp.zeros((D,), jnp.float32)}
        return inp
    _L0_xattn_all = _L0_xattn_setup()
    _L0_xattn_in = {k: v for k, v in _L0_xattn_all.items() if k in ('Wq1', 'Wk1', 'Wv1', 'Wq2', 'Wk2', 'Wv2', 'ln1_g', 'ln1_b', 'ln2_g', 'ln2_b', 'ln3_g', 'ln3_b', 'fc1_w', 'fc1_b', 'fc2_w', 'fc2_b')}
    del _L0_xattn_all

    def _L1_xattn_setup():
        import jax, jax.numpy as jnp
        import numpy as np
        import math
        E = 128
        H = 16
        DK = 64
        DV = 64
        B = 2
        S = 256
        NEG_INF = float('-inf')

        def _layer_norm(x, gamma, beta, eps=1e-12):
            mean = x.mean(-1, keepdims=True)
            var = ((x - mean) ** 2).mean(-1, keepdims=True)
            return gamma * (x - mean) / jnp.sqrt(var + eps) + beta

        def _mha(q_in, k_in, v_in, wq, bq, wk, bk, wv, bv, wo, bo, padding_mask, causal):
            Bq, Sq, _ = q_in.shape
            Sk = k_in.shape[1]
            q = (q_in @ wq + bq).reshape(Bq, Sq, H, DK).transpose(0, 2, 1, 3)
            k = (k_in @ wk + bk).reshape(Bq, Sk, H, DK).transpose(0, 2, 1, 3)
            v = (v_in @ wv + bv).reshape(Bq, Sk, H, DV).transpose(0, 2, 1, 3)
            scores = jnp.einsum('bhqd,bhkd->bhqk', q, k)
            if causal:
                causal_mask = jnp.triu(jnp.ones((Sq, Sk), dtype=bool), k=1)
                scores = jnp.where(causal_mask[None, None], NEG_INF, scores)
            if padding_mask is not None:
                scores = jnp.where(padding_mask[:, None, None, :], scores, NEG_INF)
            attn = jax.nn.softmax(scores / math.sqrt(DK), axis=-1)
            attn = jnp.nan_to_num(attn, nan=0.0, posinf=0.0, neginf=0.0)
            out = jnp.einsum('bhqk,bhkd->bhqd', attn, v)
            out = out.transpose(0, 2, 1, 3).reshape(Bq, Sq, H * DV)
            return out @ wo + bo
        key = jax.random.key(seed)
        ks = jax.random.split(key, 24)
        s = 0.02

        def w(i, shape):
            return (s * jax.random.normal(ks[i], shape)).astype(jnp.float32)
        inp = {'input': jax.random.normal(ks[0], (B, S, E), dtype=jnp.float32), 'encoder_output': jax.random.normal(ks[1], (B, S, E), dtype=jnp.float32), 'src_mask': jnp.ones((B, S), dtype=bool), 'trg_mask': jnp.ones((B, S), dtype=bool), 'sa_wq': w(2, (E, H * DK)), 'sa_bq': jnp.zeros((H * DK,), jnp.float32), 'sa_wk': w(3, (E, H * DK)), 'sa_bk': jnp.zeros((H * DK,), jnp.float32), 'sa_wv': w(4, (E, H * DV)), 'sa_bv': jnp.zeros((H * DV,), jnp.float32), 'sa_wo': w(5, (H * DV, E)), 'sa_bo': jnp.zeros((E,), jnp.float32), 'ca_wq': w(6, (E, H * DK)), 'ca_bq': jnp.zeros((H * DK,), jnp.float32), 'ca_wk': w(7, (E, H * DK)), 'ca_bk': jnp.zeros((H * DK,), jnp.float32), 'ca_wv': w(8, (E, H * DV)), 'ca_bv': jnp.zeros((H * DV,), jnp.float32), 'ca_wo': w(9, (H * DV, E)), 'ca_bo': jnp.zeros((E,), jnp.float32), 'ffn_w1': w(10, (E, 4 * E)), 'ffn_b1': jnp.zeros((4 * E,), jnp.float32), 'ffn_w2': w(11, (4 * E, E)), 'ffn_b2': jnp.zeros((E,), jnp.float32), 'ln1_g': jnp.ones((E,), jnp.float32), 'ln1_b': jnp.zeros((E,), jnp.float32), 'ln2_g': jnp.ones((E,), jnp.float32), 'ln2_b': jnp.zeros((E,), jnp.float32), 'ln3_g': jnp.ones((E,), jnp.float32), 'ln3_b': jnp.zeros((E,), jnp.float32)}
        return inp
    _L1_xattn_all = _L1_xattn_setup()
    _L1_xattn_in = {k: v for k, v in _L1_xattn_all.items() if k in ('sa_wq', 'sa_bq', 'sa_wk', 'sa_bk', 'sa_wv', 'sa_bv', 'sa_wo', 'sa_bo', 'ca_wq', 'ca_bq', 'ca_wk', 'ca_bk', 'ca_wv', 'ca_bv', 'ca_wo', 'ca_bo', 'ffn_w1', 'ffn_b1', 'ffn_w2', 'ffn_b2', 'ln1_g', 'ln1_b', 'ln2_g', 'ln2_b', 'ln3_g', 'ln3_b')}
    del _L1_xattn_all

    def _L2_xattn_setup():
        import jax, jax.numpy as jnp
        import numpy as np
        B, LX, LY = (2, 256, 256)
        E, H = (128, 16)
        HD = E // H
        FF = 512
        EPS = 1e-05

        def _rope_tables(L, d):
            inv = 1.0 / 10000.0 ** (jnp.arange(0, d, 2, dtype=jnp.float32) / d)
            t = jnp.arange(L, dtype=jnp.float32)
            f = jnp.outer(t, inv)
            return (jnp.cos(f), jnp.sin(f))

        def _apply_rope(x, cos, sin):
            d2 = x.shape[-1] // 2
            x1, x2 = (x[..., :d2], x[..., d2:])
            c = cos[None, :, None, :]
            s = sin[None, :, None, :]
            return jnp.concatenate([x1 * c - x2 * s, x2 * c + x1 * s], axis=-1)

        def _ln(x, g, b):
            m = jnp.mean(x, axis=-1, keepdims=True)
            v = jnp.var(x, axis=-1, keepdims=True)
            return (x - m) / jnp.sqrt(v + EPS) * g + b

        def _attn(q, k, v, causal):
            s = jnp.einsum('blhd,bmhd->bhlm', q, k)
            if causal:
                Lq, Lk = (s.shape[2], s.shape[3])
                mask = jnp.tril(jnp.ones((Lq, Lk), dtype=bool))
                s = jnp.where(mask, s, -jnp.inf)
            p = jax.nn.softmax(s, axis=-1)
            return jnp.einsum('bhlm,bmhd->blhd', p, v)

        def _forward(x, y, ln1_g, ln1_b, sa_wq, sa_bq, sa_wk, sa_bk, sa_wv, sa_bv, sa_wo, sa_bo, ln2_g, ln2_b, ca_wq, ca_bq, ca_wk, ca_bk, ca_wv, ca_bv, ca_wo, ca_bo, ln3_g, ln3_b, fc1_w, fc1_b, fc2_w, fc2_b):
            Bx, Lx, _ = x.shape
            Ly = y.shape[1]
            cos, sin = _rope_tables(max(Lx, Ly), HD)
            scale = HD ** (-0.5)
            h = _ln(x, ln1_g, ln1_b)
            q = (h @ sa_wq + sa_bq).reshape(Bx, Lx, H, HD) * scale
            k = (h @ sa_wk + sa_bk).reshape(Bx, Lx, H, HD)
            v = (h @ sa_wv + sa_bv).reshape(Bx, Lx, H, HD)
            q = _apply_rope(q, cos[:Lx], sin[:Lx])
            k = _apply_rope(k, cos[:Lx], sin[:Lx])
            a = _attn(q, k, v, causal=True).reshape(Bx, Lx, E)
            x = x + (a @ sa_wo + sa_bo)
            h = _ln(x, ln2_g, ln2_b)
            q = (h @ ca_wq + ca_bq).reshape(Bx, Lx, H, HD) * scale
            k = (y @ ca_wk + ca_bk).reshape(Bx, Ly, H, HD)
            v = (y @ ca_wv + ca_bv).reshape(Bx, Ly, H, HD)
            q = _apply_rope(q, cos[:Lx], sin[:Lx])
            k = _apply_rope(k, cos[:Ly], sin[:Ly])
            a = _attn(q, k, v, causal=False).reshape(Bx, Lx, E)
            x = x + (a @ ca_wo + ca_bo)
            h = _ln(x, ln3_g, ln3_b)
            return x + (jax.nn.gelu(h @ fc1_w + fc1_b) @ fc2_w + fc2_b)
        key = jax.random.key(seed)
        ks = jax.random.split(key, 16)

        def w(k, *s):
            return jax.random.normal(k, s, jnp.float32) * 0.02
        z = lambda *s: jnp.zeros(s, jnp.float32)
        o = lambda *s: jnp.ones(s, jnp.float32)
        return {'x': jax.random.normal(ks[0], (B, LX, E), jnp.float32), 'y': jax.random.normal(ks[1], (B, LY, E), jnp.float32), 'ln1_g': o(E), 'ln1_b': z(E), 'sa_wq': w(ks[2], E, E), 'sa_bq': z(E), 'sa_wk': w(ks[3], E, E), 'sa_bk': z(E), 'sa_wv': w(ks[4], E, E), 'sa_bv': z(E), 'sa_wo': w(ks[5], E, E), 'sa_bo': z(E), 'ln2_g': o(E), 'ln2_b': z(E), 'ca_wq': w(ks[6], E, E), 'ca_bq': z(E), 'ca_wk': w(ks[7], E, E), 'ca_bk': z(E), 'ca_wv': w(ks[8], E, E), 'ca_bv': z(E), 'ca_wo': w(ks[9], E, E), 'ca_bo': z(E), 'ln3_g': o(E), 'ln3_b': z(E), 'fc1_w': w(ks[10], E, FF), 'fc1_b': z(FF), 'fc2_w': w(ks[11], FF, E), 'fc2_b': z(E)}
    _L2_xattn_all = _L2_xattn_setup()
    _L2_xattn_in = {k: v for k, v in _L2_xattn_all.items() if k in ('ln1_g', 'ln1_b', 'sa_wq', 'sa_bq', 'sa_wk', 'sa_bk', 'sa_wv', 'sa_bv', 'sa_wo', 'sa_bo', 'ln2_g', 'ln2_b', 'ca_wq', 'ca_bq', 'ca_wk', 'ca_bk', 'ca_wv', 'ca_bv', 'ca_wo', 'ca_bo', 'ln3_g', 'ln3_b', 'fc1_w', 'fc1_b', 'fc2_w', 'fc2_b')}
    del _L2_xattn_all

    def _L3_xattn_setup():
        import jax, jax.numpy as jnp
        import numpy as np
        D, H, E, K, DFF = (128, 16, 8, 2, 512)
        B, L, T = (4, 64, 256)
        EPS = 1e-05

        def _xavier(key, shape):
            fan_in, fan_out = (shape[-1], shape[-2])
            a = jnp.sqrt(6.0 / (fan_in + fan_out))
            return jax.random.uniform(key, shape, jnp.float32, -a, a)

        def _ln(x, g, b):
            m = x.mean(-1, keepdims=True)
            v = ((x - m) ** 2).mean(-1, keepdims=True)
            return (x - m) / jnp.sqrt(v + EPS) * g + b

        def _mha(q_in, kv_in, in_w, in_b, out_w, out_b):
            wq, wk, wv = jnp.split(in_w, 3, axis=0)
            bq, bk, bv = jnp.split(in_b, 3, axis=0)
            dh = D // H

            def heads(x, w, b):
                y = x @ w.T + b
                return y.reshape(x.shape[0], x.shape[1], H, dh).transpose(0, 2, 1, 3)
            q = heads(q_in, wq, bq)
            k = heads(kv_in, wk, bk)
            v = heads(kv_in, wv, bv)
            scores = jnp.einsum('bhqd,bhkd->bhqk', q, k) / jnp.sqrt(jnp.float32(dh))
            attn = jax.nn.softmax(scores, axis=-1)
            out = jnp.einsum('bhqk,bhkd->bhqd', attn, v)
            out = out.transpose(0, 2, 1, 3).reshape(q_in.shape[0], q_in.shape[1], D)
            return out @ out_w.T + out_b

        def _fuse_moe(x, ln_g, ln_b, rw, rb, fc1_w, fc1_b, fc2_w, fc2_b):
            h = _ln(x, ln_g, ln_b)
            logits = h @ rw.T + rb
            vals, idx = jax.lax.top_k(logits, K)
            gates = jax.nn.softmax(vals, axis=-1)
            N = x.shape[0] * x.shape[1]
            hf = h.reshape(N, D)
            h1 = jax.nn.gelu(jnp.einsum('nd,efd->enf', hf, fc1_w) + fc1_b[:, None, :], approximate=False)
            eo = jnp.einsum('enf,edf->end', h1, fc2_w) + fc2_b[:, None, :]
            idx_f = idx.reshape(N, K)
            gates_f = gates.reshape(N, K)
            gathered = eo[idx_f, jnp.arange(N)[:, None], :]
            mixed = (gathered * gates_f[..., None]).sum(axis=1).reshape(x.shape)
            return x + mixed
        key = jax.random.key(seed)
        ks = jax.random.split(key, 16)
        inp = {'latents': jax.random.normal(ks[0], (B, L, D), jnp.float32), 'tokens': jax.random.normal(ks[1], (B, T, D), jnp.float32), 'sa_ln_g': jnp.ones((D,)), 'sa_ln_b': jnp.zeros((D,)), 'sa_in_w': _xavier(ks[2], (3 * D, D)), 'sa_in_b': jnp.zeros((3 * D,)), 'sa_out_w': _xavier(ks[3], (D, D)), 'sa_out_b': jnp.zeros((D,)), 'ca_q_ln_g': jnp.ones((D,)), 'ca_q_ln_b': jnp.zeros((D,)), 'ca_kv_ln_g': jnp.ones((D,)), 'ca_kv_ln_b': jnp.zeros((D,)), 'ca_in_w': _xavier(ks[4], (3 * D, D)), 'ca_in_b': jnp.zeros((3 * D,)), 'ca_out_w': _xavier(ks[5], (D, D)), 'ca_out_b': jnp.zeros((D,)), 'moe_ln_g': jnp.ones((D,)), 'moe_ln_b': jnp.zeros((D,)), 'router_w': _xavier(ks[6], (E, D)), 'router_b': jnp.zeros((E,)), 'e_fc1_w': jax.vmap(lambda k: _xavier(k, (DFF, D)))(jax.random.split(ks[7], E)), 'e_fc1_b': jnp.zeros((E, DFF)), 'e_fc2_w': jax.vmap(lambda k: _xavier(k, (D, DFF)))(jax.random.split(ks[8], E)), 'e_fc2_b': jnp.zeros((E, D))}
        return inp
    _L3_xattn_all = _L3_xattn_setup()
    _L3_xattn_in = {k: v for k, v in _L3_xattn_all.items() if k in ('sa_ln_g', 'sa_ln_b', 'sa_in_w', 'sa_in_b', 'sa_out_w', 'sa_out_b', 'ca_q_ln_g', 'ca_q_ln_b', 'ca_kv_ln_g', 'ca_kv_ln_b', 'ca_in_w', 'ca_in_b', 'ca_out_w', 'ca_out_b', 'moe_ln_g', 'moe_ln_b', 'router_w', 'router_b', 'e_fc1_w', 'e_fc1_b', 'e_fc2_w', 'e_fc2_b')}
    del _L3_xattn_all
    return {'x': x, 'ctx_1024': ctx_1024, 'mask_BxS2_bf1': mask_BxS2_bf1, 'L0_xattn_Wq1': _L0_xattn_in['Wq1'], 'L0_xattn_Wk1': _L0_xattn_in['Wk1'], 'L0_xattn_Wv1': _L0_xattn_in['Wv1'], 'L0_xattn_Wq2': _L0_xattn_in['Wq2'], 'L0_xattn_Wk2': _L0_xattn_in['Wk2'], 'L0_xattn_Wv2': _L0_xattn_in['Wv2'], 'L0_xattn_ln1_g': _L0_xattn_in['ln1_g'], 'L0_xattn_ln1_b': _L0_xattn_in['ln1_b'], 'L0_xattn_ln2_g': _L0_xattn_in['ln2_g'], 'L0_xattn_ln2_b': _L0_xattn_in['ln2_b'], 'L0_xattn_ln3_g': _L0_xattn_in['ln3_g'], 'L0_xattn_ln3_b': _L0_xattn_in['ln3_b'], 'L0_xattn_fc1_w': _L0_xattn_in['fc1_w'], 'L0_xattn_fc1_b': _L0_xattn_in['fc1_b'], 'L0_xattn_fc2_w': _L0_xattn_in['fc2_w'], 'L0_xattn_fc2_b': _L0_xattn_in['fc2_b'], 'L1_xattn_sa_wq': _L1_xattn_in['sa_wq'], 'L1_xattn_sa_bq': _L1_xattn_in['sa_bq'], 'L1_xattn_sa_wk': _L1_xattn_in['sa_wk'], 'L1_xattn_sa_bk': _L1_xattn_in['sa_bk'], 'L1_xattn_sa_wv': _L1_xattn_in['sa_wv'], 'L1_xattn_sa_bv': _L1_xattn_in['sa_bv'], 'L1_xattn_sa_wo': _L1_xattn_in['sa_wo'], 'L1_xattn_sa_bo': _L1_xattn_in['sa_bo'], 'L1_xattn_ca_wq': _L1_xattn_in['ca_wq'], 'L1_xattn_ca_bq': _L1_xattn_in['ca_bq'], 'L1_xattn_ca_wk': _L1_xattn_in['ca_wk'], 'L1_xattn_ca_bk': _L1_xattn_in['ca_bk'], 'L1_xattn_ca_wv': _L1_xattn_in['ca_wv'], 'L1_xattn_ca_bv': _L1_xattn_in['ca_bv'], 'L1_xattn_ca_wo': _L1_xattn_in['ca_wo'], 'L1_xattn_ca_bo': _L1_xattn_in['ca_bo'], 'L1_xattn_ffn_w1': _L1_xattn_in['ffn_w1'], 'L1_xattn_ffn_b1': _L1_xattn_in['ffn_b1'], 'L1_xattn_ffn_w2': _L1_xattn_in['ffn_w2'], 'L1_xattn_ffn_b2': _L1_xattn_in['ffn_b2'], 'L1_xattn_ln1_g': _L1_xattn_in['ln1_g'], 'L1_xattn_ln1_b': _L1_xattn_in['ln1_b'], 'L1_xattn_ln2_g': _L1_xattn_in['ln2_g'], 'L1_xattn_ln2_b': _L1_xattn_in['ln2_b'], 'L1_xattn_ln3_g': _L1_xattn_in['ln3_g'], 'L1_xattn_ln3_b': _L1_xattn_in['ln3_b'], 'L2_xattn_ln1_g': _L2_xattn_in['ln1_g'], 'L2_xattn_ln1_b': _L2_xattn_in['ln1_b'], 'L2_xattn_sa_wq': _L2_xattn_in['sa_wq'], 'L2_xattn_sa_bq': _L2_xattn_in['sa_bq'], 'L2_xattn_sa_wk': _L2_xattn_in['sa_wk'], 'L2_xattn_sa_bk': _L2_xattn_in['sa_bk'], 'L2_xattn_sa_wv': _L2_xattn_in['sa_wv'], 'L2_xattn_sa_bv': _L2_xattn_in['sa_bv'], 'L2_xattn_sa_wo': _L2_xattn_in['sa_wo'], 'L2_xattn_sa_bo': _L2_xattn_in['sa_bo'], 'L2_xattn_ln2_g': _L2_xattn_in['ln2_g'], 'L2_xattn_ln2_b': _L2_xattn_in['ln2_b'], 'L2_xattn_ca_wq': _L2_xattn_in['ca_wq'], 'L2_xattn_ca_bq': _L2_xattn_in['ca_bq'], 'L2_xattn_ca_wk': _L2_xattn_in['ca_wk'], 'L2_xattn_ca_bk': _L2_xattn_in['ca_bk'], 'L2_xattn_ca_wv': _L2_xattn_in['ca_wv'], 'L2_xattn_ca_bv': _L2_xattn_in['ca_bv'], 'L2_xattn_ca_wo': _L2_xattn_in['ca_wo'], 'L2_xattn_ca_bo': _L2_xattn_in['ca_bo'], 'L2_xattn_ln3_g': _L2_xattn_in['ln3_g'], 'L2_xattn_ln3_b': _L2_xattn_in['ln3_b'], 'L2_xattn_fc1_w': _L2_xattn_in['fc1_w'], 'L2_xattn_fc1_b': _L2_xattn_in['fc1_b'], 'L2_xattn_fc2_w': _L2_xattn_in['fc2_w'], 'L2_xattn_fc2_b': _L2_xattn_in['fc2_b'], 'L3_xattn_sa_ln_g': _L3_xattn_in['sa_ln_g'], 'L3_xattn_sa_ln_b': _L3_xattn_in['sa_ln_b'], 'L3_xattn_sa_in_w': _L3_xattn_in['sa_in_w'], 'L3_xattn_sa_in_b': _L3_xattn_in['sa_in_b'], 'L3_xattn_sa_out_w': _L3_xattn_in['sa_out_w'], 'L3_xattn_sa_out_b': _L3_xattn_in['sa_out_b'], 'L3_xattn_ca_q_ln_g': _L3_xattn_in['ca_q_ln_g'], 'L3_xattn_ca_q_ln_b': _L3_xattn_in['ca_q_ln_b'], 'L3_xattn_ca_kv_ln_g': _L3_xattn_in['ca_kv_ln_g'], 'L3_xattn_ca_kv_ln_b': _L3_xattn_in['ca_kv_ln_b'], 'L3_xattn_ca_in_w': _L3_xattn_in['ca_in_w'], 'L3_xattn_ca_in_b': _L3_xattn_in['ca_in_b'], 'L3_xattn_ca_out_w': _L3_xattn_in['ca_out_w'], 'L3_xattn_ca_out_b': _L3_xattn_in['ca_out_b'], 'L3_xattn_moe_ln_g': _L3_xattn_in['moe_ln_g'], 'L3_xattn_moe_ln_b': _L3_xattn_in['moe_ln_b'], 'L3_xattn_router_w': _L3_xattn_in['router_w'], 'L3_xattn_router_b': _L3_xattn_in['router_b'], 'L3_xattn_e_fc1_w': _L3_xattn_in['e_fc1_w'], 'L3_xattn_e_fc1_b': _L3_xattn_in['e_fc1_b'], 'L3_xattn_e_fc2_w': _L3_xattn_in['e_fc2_w'], 'L3_xattn_e_fc2_b': _L3_xattn_in['e_fc2_b']}

def reference(x, ctx_1024, mask_BxS2_bf1, L0_xattn_Wq1, L0_xattn_Wk1, L0_xattn_Wv1, L0_xattn_Wq2, L0_xattn_Wk2, L0_xattn_Wv2, L0_xattn_ln1_g, L0_xattn_ln1_b, L0_xattn_ln2_g, L0_xattn_ln2_b, L0_xattn_ln3_g, L0_xattn_ln3_b, L0_xattn_fc1_w, L0_xattn_fc1_b, L0_xattn_fc2_w, L0_xattn_fc2_b, L1_xattn_sa_wq, L1_xattn_sa_bq, L1_xattn_sa_wk, L1_xattn_sa_bk, L1_xattn_sa_wv, L1_xattn_sa_bv, L1_xattn_sa_wo, L1_xattn_sa_bo, L1_xattn_ca_wq, L1_xattn_ca_bq, L1_xattn_ca_wk, L1_xattn_ca_bk, L1_xattn_ca_wv, L1_xattn_ca_bv, L1_xattn_ca_wo, L1_xattn_ca_bo, L1_xattn_ffn_w1, L1_xattn_ffn_b1, L1_xattn_ffn_w2, L1_xattn_ffn_b2, L1_xattn_ln1_g, L1_xattn_ln1_b, L1_xattn_ln2_g, L1_xattn_ln2_b, L1_xattn_ln3_g, L1_xattn_ln3_b, L2_xattn_ln1_g, L2_xattn_ln1_b, L2_xattn_sa_wq, L2_xattn_sa_bq, L2_xattn_sa_wk, L2_xattn_sa_bk, L2_xattn_sa_wv, L2_xattn_sa_bv, L2_xattn_sa_wo, L2_xattn_sa_bo, L2_xattn_ln2_g, L2_xattn_ln2_b, L2_xattn_ca_wq, L2_xattn_ca_bq, L2_xattn_ca_wk, L2_xattn_ca_bk, L2_xattn_ca_wv, L2_xattn_ca_bv, L2_xattn_ca_wo, L2_xattn_ca_bo, L2_xattn_ln3_g, L2_xattn_ln3_b, L2_xattn_fc1_w, L2_xattn_fc1_b, L2_xattn_fc2_w, L2_xattn_fc2_b, L3_xattn_sa_ln_g, L3_xattn_sa_ln_b, L3_xattn_sa_in_w, L3_xattn_sa_in_b, L3_xattn_sa_out_w, L3_xattn_sa_out_b, L3_xattn_ca_q_ln_g, L3_xattn_ca_q_ln_b, L3_xattn_ca_kv_ln_g, L3_xattn_ca_kv_ln_b, L3_xattn_ca_in_w, L3_xattn_ca_in_b, L3_xattn_ca_out_w, L3_xattn_ca_out_b, L3_xattn_moe_ln_g, L3_xattn_moe_ln_b, L3_xattn_router_w, L3_xattn_router_b, L3_xattn_e_fc1_w, L3_xattn_e_fc1_b, L3_xattn_e_fc2_w, L3_xattn_e_fc2_b):
    import jax
    import jax.numpy as jnp

    def _L0_xattn_ref(x, context, Wq1, Wk1, Wv1, Wq2, Wk2, Wv2, ln1_g, ln1_b, ln2_g, ln2_b, ln3_g, ln3_b, fc1_w, fc1_b, fc2_w, fc2_b):
        import jax, jax.numpy as jnp
        import numpy as np
        EPS = 1e-05

        def _layernorm(x, g, b):
            m = jnp.mean(x, axis=-1, keepdims=True)
            v = jnp.mean((x - m) ** 2, axis=-1, keepdims=True)
            return (x - m) / jnp.sqrt(v + EPS) * g + b

        def _mha(x, kv, Wq, Wk, Wv, mask, causal):
            m = mask[:, None]
            Q = jnp.einsum('bsd,hdk->bhsk', x, Wq) * m
            K = jnp.einsum('bsd,hdk->bhsk', kv, Wk) * m
            V = jnp.einsum('bsd,hdk->bhsk', kv, Wv) * m
            energy = jnp.einsum('bhsk,bhtk->bhst', Q, K)
            S = energy.shape[-1]
            lengths = jnp.sum(energy[:, :, 0, :] != 0, axis=-1)
            cols = jnp.arange(S)
            energy = jnp.where(cols[None, None, None, :] >= lengths[:, :, None, None], -jnp.inf, energy)
            if causal:
                energy = jnp.where(cols[None, :] > cols[:, None], -jnp.inf, energy)
            dk = Wq.shape[-1]
            score = jax.nn.softmax(energy / jnp.sqrt(jnp.asarray(dk, energy.dtype)), axis=-1)
            out = jnp.einsum('bhst,bhtk->bhsk', score, V) * m
            B, H, Sx, dkk = out.shape
            return out.transpose(0, 2, 1, 3).reshape(B, Sx, H * dkk)
        mask0 = 1.0 - jnp.all(x == 0, axis=2, keepdims=True).astype(x.dtype)
        z = _mha(x, x, Wq1, Wk1, Wv1, mask0, causal=True)
        x1 = _layernorm(x + z, ln1_g, ln1_b)
        mask1 = 1.0 - jnp.all(x1 == 0, axis=2, keepdims=True).astype(x1.dtype)
        z = _mha(x1, context, Wq2, Wk2, Wv2, mask1, causal=False)
        x2 = _layernorm(x1 + z, ln2_g, ln2_b)
        z = jnp.maximum(x2 @ fc1_w.T + fc1_b, 0.0) * mask0
        z = (z @ fc2_w.T + fc2_b) * mask0
        return _layernorm(x2 + z, ln3_g, ln3_b)

    def _L1_xattn_ref(input, encoder_output, src_mask, trg_mask, sa_wq, sa_bq, sa_wk, sa_bk, sa_wv, sa_bv, sa_wo, sa_bo, ca_wq, ca_bq, ca_wk, ca_bk, ca_wv, ca_bv, ca_wo, ca_bo, ffn_w1, ffn_b1, ffn_w2, ffn_b2, ln1_g, ln1_b, ln2_g, ln2_b, ln3_g, ln3_b):
        import jax, jax.numpy as jnp
        import numpy as np
        import math
        E = 128
        H = 16
        DK = 64
        DV = 64
        B = 2
        S = 256
        NEG_INF = float('-inf')

        def _layer_norm(x, gamma, beta, eps=1e-12):
            mean = x.mean(-1, keepdims=True)
            var = ((x - mean) ** 2).mean(-1, keepdims=True)
            return gamma * (x - mean) / jnp.sqrt(var + eps) + beta

        def _mha(q_in, k_in, v_in, wq, bq, wk, bk, wv, bv, wo, bo, padding_mask, causal):
            Bq, Sq, _ = q_in.shape
            Sk = k_in.shape[1]
            q = (q_in @ wq + bq).reshape(Bq, Sq, H, DK).transpose(0, 2, 1, 3)
            k = (k_in @ wk + bk).reshape(Bq, Sk, H, DK).transpose(0, 2, 1, 3)
            v = (v_in @ wv + bv).reshape(Bq, Sk, H, DV).transpose(0, 2, 1, 3)
            scores = jnp.einsum('bhqd,bhkd->bhqk', q, k)
            if causal:
                causal_mask = jnp.triu(jnp.ones((Sq, Sk), dtype=bool), k=1)
                scores = jnp.where(causal_mask[None, None], NEG_INF, scores)
            if padding_mask is not None:
                scores = jnp.where(padding_mask[:, None, None, :], scores, NEG_INF)
            attn = jax.nn.softmax(scores / math.sqrt(DK), axis=-1)
            attn = jnp.nan_to_num(attn, nan=0.0, posinf=0.0, neginf=0.0)
            out = jnp.einsum('bhqk,bhkd->bhqd', attn, v)
            out = out.transpose(0, 2, 1, 3).reshape(Bq, Sq, H * DV)
            return out @ wo + bo
        residual = input
        sa = _mha(input, input, input, sa_wq, sa_bq, sa_wk, sa_bk, sa_wv, sa_bv, sa_wo, sa_bo, trg_mask, causal=True)
        x = _layer_norm(sa + residual, ln1_g, ln1_b)
        residual = x
        ca = _mha(x, encoder_output, encoder_output, ca_wq, ca_bq, ca_wk, ca_bk, ca_wv, ca_bv, ca_wo, ca_bo, src_mask, causal=False)
        x = _layer_norm(ca + residual, ln2_g, ln2_b)
        residual = x
        h = jax.nn.relu(x @ ffn_w1 + ffn_b1)
        x = _layer_norm(h @ ffn_w2 + ffn_b2 + residual, ln3_g, ln3_b)
        return x

    def _L2_xattn_ref(x, y, ln1_g, ln1_b, sa_wq, sa_bq, sa_wk, sa_bk, sa_wv, sa_bv, sa_wo, sa_bo, ln2_g, ln2_b, ca_wq, ca_bq, ca_wk, ca_bk, ca_wv, ca_bv, ca_wo, ca_bo, ln3_g, ln3_b, fc1_w, fc1_b, fc2_w, fc2_b):
        import jax, jax.numpy as jnp
        import numpy as np
        B, LX, LY = (2, 256, 256)
        E, H = (128, 16)
        HD = E // H
        FF = 512
        EPS = 1e-05

        def _rope_tables(L, d):
            inv = 1.0 / 10000.0 ** (jnp.arange(0, d, 2, dtype=jnp.float32) / d)
            t = jnp.arange(L, dtype=jnp.float32)
            f = jnp.outer(t, inv)
            return (jnp.cos(f), jnp.sin(f))

        def _apply_rope(x, cos, sin):
            d2 = x.shape[-1] // 2
            x1, x2 = (x[..., :d2], x[..., d2:])
            c = cos[None, :, None, :]
            s = sin[None, :, None, :]
            return jnp.concatenate([x1 * c - x2 * s, x2 * c + x1 * s], axis=-1)

        def _ln(x, g, b):
            m = jnp.mean(x, axis=-1, keepdims=True)
            v = jnp.var(x, axis=-1, keepdims=True)
            return (x - m) / jnp.sqrt(v + EPS) * g + b

        def _attn(q, k, v, causal):
            s = jnp.einsum('blhd,bmhd->bhlm', q, k)
            if causal:
                Lq, Lk = (s.shape[2], s.shape[3])
                mask = jnp.tril(jnp.ones((Lq, Lk), dtype=bool))
                s = jnp.where(mask, s, -jnp.inf)
            p = jax.nn.softmax(s, axis=-1)
            return jnp.einsum('bhlm,bmhd->blhd', p, v)

        def _forward(x, y, ln1_g, ln1_b, sa_wq, sa_bq, sa_wk, sa_bk, sa_wv, sa_bv, sa_wo, sa_bo, ln2_g, ln2_b, ca_wq, ca_bq, ca_wk, ca_bk, ca_wv, ca_bv, ca_wo, ca_bo, ln3_g, ln3_b, fc1_w, fc1_b, fc2_w, fc2_b):
            Bx, Lx, _ = x.shape
            Ly = y.shape[1]
            cos, sin = _rope_tables(max(Lx, Ly), HD)
            scale = HD ** (-0.5)
            h = _ln(x, ln1_g, ln1_b)
            q = (h @ sa_wq + sa_bq).reshape(Bx, Lx, H, HD) * scale
            k = (h @ sa_wk + sa_bk).reshape(Bx, Lx, H, HD)
            v = (h @ sa_wv + sa_bv).reshape(Bx, Lx, H, HD)
            q = _apply_rope(q, cos[:Lx], sin[:Lx])
            k = _apply_rope(k, cos[:Lx], sin[:Lx])
            a = _attn(q, k, v, causal=True).reshape(Bx, Lx, E)
            x = x + (a @ sa_wo + sa_bo)
            h = _ln(x, ln2_g, ln2_b)
            q = (h @ ca_wq + ca_bq).reshape(Bx, Lx, H, HD) * scale
            k = (y @ ca_wk + ca_bk).reshape(Bx, Ly, H, HD)
            v = (y @ ca_wv + ca_bv).reshape(Bx, Ly, H, HD)
            q = _apply_rope(q, cos[:Lx], sin[:Lx])
            k = _apply_rope(k, cos[:Ly], sin[:Ly])
            a = _attn(q, k, v, causal=False).reshape(Bx, Lx, E)
            x = x + (a @ ca_wo + ca_bo)
            h = _ln(x, ln3_g, ln3_b)
            return x + (jax.nn.gelu(h @ fc1_w + fc1_b) @ fc2_w + fc2_b)
        return _forward(x, y, ln1_g, ln1_b, sa_wq, sa_bq, sa_wk, sa_bk, sa_wv, sa_bv, sa_wo, sa_bo, ln2_g, ln2_b, ca_wq, ca_bq, ca_wk, ca_bk, ca_wv, ca_bv, ca_wo, ca_bo, ln3_g, ln3_b, fc1_w, fc1_b, fc2_w, fc2_b)

    def _L3_xattn_ref(latents, tokens, sa_ln_g, sa_ln_b, sa_in_w, sa_in_b, sa_out_w, sa_out_b, ca_q_ln_g, ca_q_ln_b, ca_kv_ln_g, ca_kv_ln_b, ca_in_w, ca_in_b, ca_out_w, ca_out_b, moe_ln_g, moe_ln_b, router_w, router_b, e_fc1_w, e_fc1_b, e_fc2_w, e_fc2_b):
        import jax, jax.numpy as jnp
        import numpy as np
        D, H, E, K, DFF = (128, 16, 8, 2, 512)
        B, L, T = (4, 64, 256)
        EPS = 1e-05

        def _xavier(key, shape):
            fan_in, fan_out = (shape[-1], shape[-2])
            a = jnp.sqrt(6.0 / (fan_in + fan_out))
            return jax.random.uniform(key, shape, jnp.float32, -a, a)

        def _ln(x, g, b):
            m = x.mean(-1, keepdims=True)
            v = ((x - m) ** 2).mean(-1, keepdims=True)
            return (x - m) / jnp.sqrt(v + EPS) * g + b

        def _mha(q_in, kv_in, in_w, in_b, out_w, out_b):
            wq, wk, wv = jnp.split(in_w, 3, axis=0)
            bq, bk, bv = jnp.split(in_b, 3, axis=0)
            dh = D // H

            def heads(x, w, b):
                y = x @ w.T + b
                return y.reshape(x.shape[0], x.shape[1], H, dh).transpose(0, 2, 1, 3)
            q = heads(q_in, wq, bq)
            k = heads(kv_in, wk, bk)
            v = heads(kv_in, wv, bv)
            scores = jnp.einsum('bhqd,bhkd->bhqk', q, k) / jnp.sqrt(jnp.float32(dh))
            attn = jax.nn.softmax(scores, axis=-1)
            out = jnp.einsum('bhqk,bhkd->bhqd', attn, v)
            out = out.transpose(0, 2, 1, 3).reshape(q_in.shape[0], q_in.shape[1], D)
            return out @ out_w.T + out_b

        def _fuse_moe(x, ln_g, ln_b, rw, rb, fc1_w, fc1_b, fc2_w, fc2_b):
            h = _ln(x, ln_g, ln_b)
            logits = h @ rw.T + rb
            vals, idx = jax.lax.top_k(logits, K)
            gates = jax.nn.softmax(vals, axis=-1)
            N = x.shape[0] * x.shape[1]
            hf = h.reshape(N, D)
            h1 = jax.nn.gelu(jnp.einsum('nd,efd->enf', hf, fc1_w) + fc1_b[:, None, :], approximate=False)
            eo = jnp.einsum('enf,edf->end', h1, fc2_w) + fc2_b[:, None, :]
            idx_f = idx.reshape(N, K)
            gates_f = gates.reshape(N, K)
            gathered = eo[idx_f, jnp.arange(N)[:, None], :]
            mixed = (gathered * gates_f[..., None]).sum(axis=1).reshape(x.shape)
            return x + mixed
        q = _ln(latents, sa_ln_g, sa_ln_b)
        x = latents + _mha(q, q, sa_in_w, sa_in_b, sa_out_w, sa_out_b)
        qc = _ln(x, ca_q_ln_g, ca_q_ln_b)
        kv = _ln(tokens, ca_kv_ln_g, ca_kv_ln_b)
        x = x + _mha(qc, kv, ca_in_w, ca_in_b, ca_out_w, ca_out_b)
        return _fuse_moe(x, moe_ln_g, moe_ln_b, router_w, router_b, e_fc1_w, e_fc1_b, e_fc2_w, e_fc2_b)
    x = _L0_xattn_ref(x, ctx_1024, L0_xattn_Wq1, L0_xattn_Wk1, L0_xattn_Wv1, L0_xattn_Wq2, L0_xattn_Wk2, L0_xattn_Wv2, L0_xattn_ln1_g, L0_xattn_ln1_b, L0_xattn_ln2_g, L0_xattn_ln2_b, L0_xattn_ln3_g, L0_xattn_ln3_b, L0_xattn_fc1_w, L0_xattn_fc1_b, L0_xattn_fc2_w, L0_xattn_fc2_b)
    x = _L1_xattn_ref(x, ctx_1024, mask_BxS2_bf1, mask_BxS2_bf1, L1_xattn_sa_wq, L1_xattn_sa_bq, L1_xattn_sa_wk, L1_xattn_sa_bk, L1_xattn_sa_wv, L1_xattn_sa_bv, L1_xattn_sa_wo, L1_xattn_sa_bo, L1_xattn_ca_wq, L1_xattn_ca_bq, L1_xattn_ca_wk, L1_xattn_ca_bk, L1_xattn_ca_wv, L1_xattn_ca_bv, L1_xattn_ca_wo, L1_xattn_ca_bo, L1_xattn_ffn_w1, L1_xattn_ffn_b1, L1_xattn_ffn_w2, L1_xattn_ffn_b2, L1_xattn_ln1_g, L1_xattn_ln1_b, L1_xattn_ln2_g, L1_xattn_ln2_b, L1_xattn_ln3_g, L1_xattn_ln3_b)
    x = _L2_xattn_ref(x, ctx_1024, L2_xattn_ln1_g, L2_xattn_ln1_b, L2_xattn_sa_wq, L2_xattn_sa_bq, L2_xattn_sa_wk, L2_xattn_sa_bk, L2_xattn_sa_wv, L2_xattn_sa_bv, L2_xattn_sa_wo, L2_xattn_sa_bo, L2_xattn_ln2_g, L2_xattn_ln2_b, L2_xattn_ca_wq, L2_xattn_ca_bq, L2_xattn_ca_wk, L2_xattn_ca_bk, L2_xattn_ca_wv, L2_xattn_ca_bv, L2_xattn_ca_wo, L2_xattn_ca_bo, L2_xattn_ln3_g, L2_xattn_ln3_b, L2_xattn_fc1_w, L2_xattn_fc1_b, L2_xattn_fc2_w, L2_xattn_fc2_b)
    x = _L3_xattn_ref(x, ctx_1024, L3_xattn_sa_ln_g, L3_xattn_sa_ln_b, L3_xattn_sa_in_w, L3_xattn_sa_in_b, L3_xattn_sa_out_w, L3_xattn_sa_out_b, L3_xattn_ca_q_ln_g, L3_xattn_ca_q_ln_b, L3_xattn_ca_kv_ln_g, L3_xattn_ca_kv_ln_b, L3_xattn_ca_in_w, L3_xattn_ca_in_b, L3_xattn_ca_out_w, L3_xattn_ca_out_b, L3_xattn_moe_ln_g, L3_xattn_moe_ln_b, L3_xattn_router_w, L3_xattn_router_b, L3_xattn_e_fc1_w, L3_xattn_e_fc1_b, L3_xattn_e_fc2_w, L3_xattn_e_fc2_b)
    return x

_drawn_inputs = setup_inputs


def setup_inputs(seed=0):
    import zlib

    import numpy as np

    out = dict(_drawn_inputs(seed))
    spreads = {'L0_xattn_ln1_g': (1.0, 0.2),
     'L0_xattn_ln1_b': (0.0, 0.1),
     'L0_xattn_ln2_g': (1.0, 0.2),
     'L0_xattn_ln2_b': (0.0, 0.1),
     'L0_xattn_ln3_g': (1.0, 0.2),
     'L0_xattn_ln3_b': (0.0, 0.1),
     'L0_xattn_fc1_b': (0.0, 0.1),
     'L0_xattn_fc2_b': (0.0, 0.1),
     'L1_xattn_sa_bq': (0.0, 0.8),
     'L1_xattn_sa_bk': (0.0, 0.8),
     'L1_xattn_sa_bv': (0.0, 0.1),
     'L1_xattn_sa_bo': (0.0, 0.1),
     'L1_xattn_ca_bq': (0.0, 0.8),
     'L1_xattn_ca_bk': (0.0, 0.8),
     'L1_xattn_ca_bv': (0.0, 0.1),
     'L1_xattn_ca_bo': (0.0, 0.1),
     'L1_xattn_ffn_b1': (0.0, 0.1),
     'L1_xattn_ffn_b2': (0.0, 0.1),
     'L1_xattn_ln1_g': (1.0, 0.2),
     'L1_xattn_ln1_b': (0.0, 0.1),
     'L1_xattn_ln2_g': (1.0, 0.2),
     'L1_xattn_ln2_b': (0.0, 0.1),
     'L1_xattn_ln3_g': (1.0, 0.2),
     'L1_xattn_ln3_b': (0.0, 0.1),
     'L2_xattn_ln1_g': (1.0, 0.6),
     'L2_xattn_ln1_b': (0.0, 0.329),
     'L2_xattn_sa_bq': (0.0, 0.8),
     'L2_xattn_sa_bk': (0.0, 0.8),
     'L2_xattn_sa_bv': (0.0, 0.1),
     'L2_xattn_sa_bo': (0.0, 0.1),
     'L2_xattn_ln2_g': (1.0, 0.6),
     'L2_xattn_ln2_b': (0.0, 0.8),
     'L2_xattn_ca_bq': (0.0, 0.8),
     'L2_xattn_ca_bk': (0.0, 0.8),
     'L2_xattn_ca_bv': (0.0, 0.1),
     'L2_xattn_ca_bo': (0.0, 0.1),
     'L2_xattn_ln3_g': (1.0, 0.574),
     'L2_xattn_ln3_b': (0.0, 0.452),
     'L2_xattn_fc1_b': (0.0, 0.1),
     'L2_xattn_fc2_b': (0.0, 0.1),
     'L3_xattn_sa_ln_g': (1.0, 0.2),
     'L3_xattn_sa_ln_b': (0.0, 0.1),
     'L3_xattn_sa_in_b': (0.0, 0.1),
     'L3_xattn_sa_out_b': (0.0, 0.1),
     'L3_xattn_ca_q_ln_g': (1.0, 0.2),
     'L3_xattn_ca_q_ln_b': (0.0, 0.39),
     'L3_xattn_ca_kv_ln_g': (1.0, 0.2),
     'L3_xattn_ca_kv_ln_b': (0.0, 0.1),
     'L3_xattn_ca_in_b': (0.0, 0.1),
     'L3_xattn_ca_out_b': (0.0, 0.1),
     'L3_xattn_moe_ln_g': (1.0, 0.2),
     'L3_xattn_moe_ln_b': (0.0, 0.1),
     'L3_xattn_router_b': (0.0, 0.1),
     'L3_xattn_e_fc1_b': (0.0, 0.1),
     'L3_xattn_e_fc2_b': (0.0, 0.1)}
    factors = {'L0_xattn_Wq1': 6.648,
     'L0_xattn_Wk1': 6.535,
     'L0_xattn_Wq2': 5.147,
     'L0_xattn_Wk2': 6.107,
     'L1_xattn_sa_wq': 7.204,
     'L1_xattn_sa_wk': 7.197,
     'L1_xattn_ca_wq': 6.926,
     'L1_xattn_ca_wk': 6.3,
     'L2_xattn_sa_wq': 8.0,
     'L2_xattn_sa_wk': 8.0,
     'L2_xattn_ca_wq': 8.0,
     'L2_xattn_ca_wk': 8.0}
    for name, (base, spread) in spreads.items():
        noise = np.random.default_rng([zlib.crc32(name.encode()), seed]).standard_normal(out[name].shape)
        drawn = base * np.exp(spread * noise) if base else spread * noise
        out[name] = jnp.asarray(drawn.astype(out[name].dtype))
    for name, factor in factors.items():
        out[name] = (out[name] * factor).astype(out[name].dtype)
    return out
```

```python
from contextlib import ExitStack

import numpy as np

import concourse.bass as bass
from concourse import mybir

P = 128
B, T, D, H = 128, 64, 128, 16
NU = 4
NS = NU // 2
TOK = NU * P
ITERS = B * T // TOK
NB = TOK // T
SB = NB // NS
SW = TOK // NS
HP = H // 2
DK = D // H
DKB = 64
FF = 512
NE = 8
BIG = 1.0e30
F32 = mybir.dt.float32
BF16 = mybir.dt.bfloat16
U8 = mybir.dt.uint8
U32 = mybir.dt.uint32
ALU = mybir.AluOpType
ACT = mybir.ActivationFunctionType
X_AXIS = mybir.AxisListType.X

SITES = [
    dict(layer=0, cross=False, causal=True, wide=False, rope=False, lengths=True, bias=False, out=False),
    dict(layer=0, cross=True, causal=False, wide=False, rope=False, lengths=True, bias=False, out=False),
    dict(layer=1, cross=False, causal=True, wide=True, rope=False, lengths=False, bias=True, out=True),
    dict(layer=1, cross=True, causal=False, wide=True, rope=False, lengths=False, bias=True, out=True),
    dict(layer=2, cross=False, causal=True, wide=False, rope=True, lengths=False, bias=True, out=True),
    dict(layer=2, cross=True, causal=False, wide=False, rope=True, lengths=False, bias=True, out=True),
    dict(layer=3, cross=False, causal=False, wide=False, rope=False, lengths=False, bias=True, out=True),
    dict(layer=3, cross=True, causal=False, wide=False, rope=False, lengths=False, bias=True, out=True),
]

NORMS = [
    dict(g="L0_xattn_ln1_g", b="L0_xattn_ln1_b", eps=1e-5, post=True, add=None),
    dict(g="L0_xattn_ln2_g", b="L0_xattn_ln2_b", eps=1e-5, post=True, add=None),
    dict(g="L0_xattn_ln3_g", b="L0_xattn_ln3_b", eps=1e-5, post=True, add="L1_xattn_sa_bo"),
    dict(g="L1_xattn_ln1_g", b="L1_xattn_ln1_b", eps=1e-12, post=True, add="L1_xattn_ca_bo"),
    dict(g="L1_xattn_ln2_g", b="L1_xattn_ln2_b", eps=1e-12, post=True, add="L1_xattn_ffn_b2"),
    dict(g="L1_xattn_ln3_g", b="L1_xattn_ln3_b", eps=1e-12, post=True, add=None),
    dict(g="L2_xattn_ln1_g", b="L2_xattn_ln1_b", eps=1e-5, post=False, add="L2_xattn_sa_bo"),
    dict(g="L2_xattn_ln2_g", b="L2_xattn_ln2_b", eps=1e-5, post=False, add="L2_xattn_ca_bo"),
    dict(g="L2_xattn_ln3_g", b="L2_xattn_ln3_b", eps=1e-5, post=False, add="L2_xattn_fc2_b"),
    dict(g="L3_xattn_sa_ln_g", b="L3_xattn_sa_ln_b", eps=1e-5, post=False, add="L3_xattn_sa_out_b"),
    dict(g="L3_xattn_ca_q_ln_g", b="L3_xattn_ca_q_ln_b", eps=1e-5, post=False, add="L3_xattn_ca_out_b"),
    dict(g="L3_xattn_moe_ln_g", b="L3_xattn_moe_ln_b", eps=1e-5, post=False, add=None),
]
CTX_NORM = dict(g="L3_xattn_ca_kv_ln_g", b="L3_xattn_ca_kv_ln_b", eps=1e-5)
AFTER_SITE = {0: 0, 1: 1, 2: 3, 3: 4, 4: 7, 5: 8, 6: 10, 7: 11}
AFTER_FFN = {0: 2, 1: 5, 2: 9}
LN_ONLY = 6
FFN_WIDTH = {0: D, 1: FF, 2: FF}


def schedule():
    steps = [("input_turn", 0), ("input_turn", 1), ("masks",)]
    left = [[], []]

    def attention(a):
        site, r = SITES[a], AFTER_SITE[a]

        def qk(s):
            turn = [("ctx_turn", a, s)] if a in (1, 3, 7) else []
            return turn + [("qk", a, s)] + ([("lengths", a, s)] if site["lengths"] else [])

        def res(u):
            out = [("out_turn", a, u)] if site["out"] else []
            return out + [("residual", a, r, u), ("norm", r, u)] + ([("ctx_mask", u)] if a == 0 else [])

        def use(u):
            return [("turn", a, u), ("pv", a, u)]

        seq = left[0] + qk(0) + [("v", a, 0)] if site["rope"] else qk(0) + [("v", a, 0)] + left[0]
        if site["wide"]:
            seq += [("scores", a, 0), ("scores", a, 1)] + left[1] + use(0) + qk(1) + [("scores", a, 2)]
            seq += use(1) + [("v", a, 1)] + res(0) + [("scores", a, 3)] + res(1)
        else:
            seq += [("scores", a, 0)] + left[1] + qk(1) + [("v", a, 1), ("scores", a, 1)] + use(0)
            seq += [("scores", a, 2)] + use(1) + res(0) + [("scores", a, 3)] + res(1)
        seq += use(2) + use(3) + [("norm_turn", r, 0)] + res(2)
        left[:] = [res(3), [("norm_turn", r, 1)]]
        return seq

    def ffn(n):
        r, last = AFTER_FFN[n], AFTER_FFN[n]

        def down(u):
            more = [("norm", LN_ONLY, u)] if n == 1 else []
            return [("ffn_down", n, u), ("norm", r, u)] + more

        if n == 1:
            last = LN_ONLY
        seq = [("ffn_up", n, 0)] + left[0] + left[1] + down(0) + [("ffn_up", n, 1)] + down(1) + down(2)
        seq += [("norm_turn", last, 0)]
        left[:] = [down(3), [("norm_turn", last, 1)]]
        return seq

    steps += attention(0) + attention(1) + ffn(0)
    steps += attention(2) + attention(3) + ffn(1)
    steps += attention(4) + attention(5) + [("ctx_norm", u) for u in range(NU)] + ffn(2)
    steps += attention(6) + attention(7)
    steps += [("route", 0), ("route", 1)] + left[0] + left[1] + [("route", 2), ("route", 3)]
    halves = [(e, s) for e in range(NE) for s in range(NS)]
    steps += [("expert_up", *halves[0]), ("expert_up", *halves[1])] + [("route_bias", u) for u in range(NU)]
    for n, (e, s) in enumerate(halves):
        steps += [("expert_down", e, s)]
        if n + 2 < len(halves):
            steps += [("expert_up", *halves[n + 2])]
    return steps



def weight_layout():
    at, n = {}, 0

    def put(name, width):
        nonlocal n
        at[name] = (n, width)
        n += width

    for a in range(8):
        wide = SITES[a]["wide"]
        w = H * DKB if wide else D
        for k in ("q", "k", "v") + (("qp", "kp") if SITES[a]["rope"] else ()):
            put(f"w{k}{a}", w)
        if SITES[a]["out"]:
            put(f"wo{a}", w)
    for n_, f in FFN_WIDTH.items():
        put(f"up{n_}", f)
        put(f"down{n_}", f)
    put("router", NE)
    for e in range(NE):
        put(f"up_e{e}", FF)
        put(f"down_e{e}", FF)
    return at, n


def column_layout():
    at, n = {}, 0

    def put(name, width):
        nonlocal n
        at[name] = (n, width)
        n += width

    for r in range(len(NORMS)):
        put(f"g{r}", 1)
        put(f"b{r}", 1)
    put("gc", 1)
    put("bc", 1)
    for a in range(8):
        if SITES[a]["bias"]:
            w = HP if SITES[a]["wide"] else 1
            for k in ("q", "k") + (("qp", "kp") if SITES[a]["rope"] else ()):
                put(f"b{k}{a}", w)
    for n_, f in FFN_WIDTH.items():
        put(f"up_b{n_}", f // P)
    for e in range(NE):
        put(f"up_be{e}", FF // P)
    return at, n


def row_layout():
    at, n = {}, 0

    def put(name, width):
        nonlocal n
        at[name] = (n, width)
        n += width

    for r, norm in enumerate(NORMS):
        if norm["post"]:
            put(f"g{r}", D)
            put(f"b{r}", D)
        if norm["add"]:
            put(f"add{r}", D)
    for a in range(8):
        if SITES[a]["bias"]:
            put(f"bv{a}", H * DKB if SITES[a]["wide"] else D)
    put("down_b0", D)
    put("router_b", NE)
    return at, n


def constant_layout():
    at, n = {}, 0
    for name, width in (("ident", P), ("head_of_four", 4), ("causal", T), ("iota", T), ("head_of_all", 32), ("own_head", H), ("own_rows", SB),
                        ("cos", SW), ("sin", SW)):
        at[name] = (n, width)
        n += width
    return at, n


W_AT, W_N = weight_layout()
C_AT, C_N = column_layout()
R_AT, R_N = row_layout()
K_AT, K_N = constant_layout()


class Ring:

    def __init__(self, banks, full, emptied):
        self.banks, self.full, self.emptied = banks, full, emptied
        self.at = {}

    def take(self, pe, name):
        n = len(self.at)
        k = n % len(self.banks)
        turn = n // len(self.banks) + 1
        self.at[name] = (k, turn)
        if turn > 1:
            pe.wait_ge(self.emptied[k], turn - 1)
        return self.banks[k]

    def filled(self, name):
        return self.full[self.at[name][0]]

    def read(self, name):
        return self.emptied[self.at[name][0]]

    def wait_filled(self, engine, name):
        k, turn = self.at[name]
        engine.wait_ge(self.full[k], turn)
        return self.banks[k]

    def wait_read(self, engine, name):
        k, turn = self.at[name]
        engine.wait_ge(self.emptied[k], turn)


def decoder_stack(nc, x, ctx, mask, weights, columns, rows, constants, expert_bias, out):
    steps = schedule()
    with ExitStack() as stack:
        def sb(name, shape, dt=F32):
            return stack.enter_context(nc.sbuf_tensor(name, shape, dt))

        def sem(name):
            return stack.enter_context(nc.semaphore(name))

        w_sb = sb("w_sb", [P, W_N])
        col = sb("col", [P, C_N])
        row = sb("row", [P, R_N])
        const = sb("const", [P, K_N])
        expert_b = sb("expert_b", [NE, D])
        res = sb("res", [P, NU, D])
        raw = sb("raw", [P, NU, D])
        normed = sb("normed", [P, NU, D])
        c_tok = sb("c_tok", [P, NU, D])
        c_work = sb("c_work", [P, NU, D])
        scaled = sb("scaled", [P, 2, D])
        hT = sb("hT", [P, TOK])
        cT = sb("cT", [P, TOK])
        qT = sb("qT", [P, TOK])
        kT = sb("kT", [P, TOK])
        k4 = sb("k4", [P, 4, TOK])
        v8 = sb("v8", [P, NB * HP, 2 * (DK + 1)])
        qW = k4[:].rearrange("p j t -> p (j t)").rearrange("p (c t) -> p c t", c=HP)
        kW = sb("kW", [P, HP, SB, P])
        vW = sb("vW", [P, SB, HP, P])
        probs = sb("probs", [P, 2, H * T])
        pT = sb("pT", [P, 2, HP, P])
        att = sb("att", [P, 2, H * DKB])
        attT = sb("attT", [P, HP, P])
        hid = att[:].rearrange("p s (f t) -> p s f t", t=SW)
        rope_a = att[:, 0, 512:1024].rearrange("p (k t) -> p k t", k=2)
        rope_b = att[:, 1, 512:1024].rearrange("p (k t) -> p k t", k=2)
        len_mask = attT[:].rearrange("p c t -> p (c t)").bitcast(BF16).rearrange("p (s w) -> p s w", s=NS)
        mask_u8 = sb("mask_u8", [P, NU, T], U8)
        pad = sb("pad", [P, NU, T])
        pad_causal = sb("pad_causal", [P, NU, T])
        top = sb("top", [P, H])
        den = sb("den", [P, H])
        first_q = sb("first_q", [P, SB, 32])
        own_rows = sb("own_rows", [P, SB, T], BF16)
        flags = sb("flags", [P, T])
        late = sb("late", [P, T])
        count = sb("count", [P, 1])
        valid = sb("valid", [P, H])
        tok_mask = sb("tok_mask", [P, 2, NU])
        stat6 = sb("stat6", [P, 6])
        stat = sb("stat", [P, NU, 2])
        log_var = sb("log_var", [P, NU])
        rstd = sb("rstd", [P, NU])
        newton = sb("newton", [P, 2])
        logits = sb("logits", [P, NU, NE])
        best = sb("best", [P, NU, NE])
        best_i = sb("best_i", [P, NU, NE], U32)
        best_f = sb("best_f", [P, NE])
        share = sb("share", [P, NU, 4])
        one_hot = sb("one_hot", [P, 2, NE])
        gates = sb("gates", [P, NU, NE])
        gatesT = pT[0:NE, 0, 0:NU, :]

        sc = stack.enter_context(nc.psum_tensor("sc", [P, 4, 512], F32))
        work = stack.enter_context(nc.psum_tensor("work", [P, 4, 512], F32))

        weights_in = sem("weights_in")
        zeroed = sem("zeroed")
        ones_set = sem("ones_set")
        x_in = sem("x_in")
        ctx_in = sem("ctx_in")
        mask_in = sem("mask_in")
        out_stored = sem("out_stored")
        k4_done = sem("k4_done")
        rope_parts = sem("rope_parts")
        rope_done = sem("rope_done")
        scores_done = sem("scores_done")
        scores_read = sem("scores_read")
        first_q_done = sem("first_q_done")
        counted = sem("counted")
        len_masked = sem("len_masked")
        shifted = sem("shifted")
        exp_done = sem("exp_done")
        stats_done = sem("stats_done")
        normed_done = sem("normed_done")
        res_done = sem("res_done")
        tok_masked = sem("tok_masked")
        ctx_masked = sem("ctx_masked")
        ctx_stats = sem("ctx_stats")
        ctx_normed = sem("ctx_normed")
        route_diff = sem("route_diff")
        route_exp = sem("route_exp")
        gates_done = sem("gates_done")
        vector_step = sem("vector_step")
        pool_step = sem("pool_step")
        scalar_step = sem("scalar_step")
        rstd_done = sem("rstd_done")
        ring = Ring([work[:, k, :] for k in range(4)], [sem(f"bank_filled{k}") for k in range(4)],
                    [sem(f"bank_read{k}") for k in range(4)])
        per_tile = [x_in, ctx_in, mask_in, out_stored, k4_done, rope_parts, rope_done, scores_done,
                    scores_read, first_q_done, counted, len_masked, shifted, exp_done, stats_done, normed_done, res_done,
                    tok_masked, ctx_masked, ctx_stats, ctx_normed, route_diff, route_exp, gates_done,
                    vector_step, pool_step, scalar_step, rstd_done, *ring.full, *ring.emptied]

        def W(name, lo=0, n=None):
            at, width = W_AT[name]
            return w_sb[:, at + lo:at + (width if n is None else lo + n)]

        def COL(name, k=0):
            return col[:, C_AT[name][0] + k:C_AT[name][0] + k + 1]

        def ROW(name, lo=0, n=None):
            at, width = R_AT[name]
            return row[:, at + lo:at + (width if n is None else lo + n)]

        def K(name, lo=0, n=None):
            at, width = K_AT[name]
            return const[:, at + lo:at + (width if n is None else lo + n)]

        ident = K("ident")

        K4_N = {x: n + 1 for n, x in enumerate([s[1:] for s in steps if s[0] == "qk" and not SITES[s[1]]["wide"]])}
        ROPE_N = {x: n + 1 for n, x in enumerate([s[1:] for s in steps if s[0] == "qk" and SITES[s[1]]["rope"]])}
        NORM_N = {x: n + 1 for n, x in enumerate([s[1:] for s in steps if s[0] == "norm"])}
        RSTD_N = {x: n + 1 for n, x in enumerate([s for s in steps if s[0] in ("norm", "ctx_norm")])}
        SHIFT_N = {x: n + 1 for n, x in enumerate([s[1:] for s in steps if s[0] == "scores" and (
            SITES[s[1]]["wide"] or SITES[s[1]]["causal"])])}
        LEN_N = {x: n + 1 for n, x in enumerate([s[1:] for s in steps if s[0] == "lengths"])}
        OUT_N = {x: n + 1 for n, x in enumerate([s[1:] for s in steps if s[0] == "out_turn"])}

        def wait_pv(engine, a, u):
            n = NU * a + u - 2
            if n >= 0:
                job = ("pv", n // NU, n % NU)
                ring.wait_filled(engine, job + (1,) if SITES[n // NU]["wide"] else job)

        def wait_att(engine, a, u):
            sites = [k for k in range(8) if SITES[k]["out"]]
            n = NU * sites.index(a) + u - 2
            pa, pu = sites[n // NU], n % NU
            ring.wait_filled(engine, ("out_turn", pa, pu, 1 if SITES[pa]["wide"] else 0))

        with nc.Block() as block:
            @block.sync
            def _(sp):
                third = W_N // 4
                for k in range(4):
                    lo, hi = third * k, W_N if k == 3 else third * (k + 1)
                    sp.dma_start(w_sb[:, lo:hi], weights[:, lo:hi]).then_inc(weights_in, 16)
                sp.dma_start(col[:], columns[:, :]).then_inc(weights_in, 16)
                sp.dma_start(row[:], rows[:, :].to_broadcast([P, R_N])).then_inc(weights_in, 16)
                sp.dma_start(const[:], constants[:, :]).then_inc(weights_in, 16)
                sp.dma_start(expert_b[:], expert_bias[:, :]).then_inc(weights_in, 16)
                sp.wait_ge(weights_in, 16 * 8)

            @block.vector
            def _(dve):
                dve.memset(kW[:], 0.0).then_inc(zeroed, 1)
                dve.memset(vW[:], 0.0).then_inc(zeroed, 1)
                dve.memset(v8[:], 0.0).then_inc(zeroed, 1)
                dve.wait_ge(zeroed, 3)
                dve.memset(v8[0:T, :, DK:DK + 1], 1.0).then_inc(ones_set, 1)
                dve.memset(v8[T:P, :, 2 * DK + 1:2 * DK + 2], 1.0).then_inc(ones_set, 1)
                dve.wait_ge(weights_in, 16 * 8)
                dve.tensor_copy(own_rows[:], K("own_rows").rearrange("p (b o) -> p b o", o=1)
                                .to_broadcast([P, SB, T])).then_inc(ones_set, 1)

        with nc.Fori(0, ITERS) as tile:
            with nc.Block() as block:

                @block.tensor
                def _(pe):
                    def kv_of(a):
                        return cT if SITES[a]["cross"] else hT

                    def wait_source(a, s):
                        ring.wait_read(pe, SOURCE[(a, "h", s)])
                        if SITES[a]["cross"]:
                            ring.wait_read(pe, SOURCE[(a, "c", s)])

                    SOURCE = {}
                    last_h = {s: ("input_turn", s) for s in range(NS)}
                    last_c = {}
                    for step in steps:
                        if step[0] == "norm_turn":
                            last_h[step[2]] = step
                        if step[0] == "ctx_turn":
                            last_c[step[2]] = step
                        if step[0] in ("qk", "v"):
                            SOURCE[(step[1], "h", step[2])] = last_h[step[2]]
                            SOURCE[(step[1], "c", step[2])] = last_c.get(step[2])

                    def turn_stream(step, src, s):
                        bank = ring.take(pe, step)
                        for j in range(2):
                            i = nc.tensor.transpose(bank[:, j * P:(j + 1) * P], src[:, 2 * s + j, :], ident)
                        i.then_inc(ring.filled(step), 1)

                    h_now = {}
                    for step in steps:
                        kind = step[0]
                        if kind == "input_turn":
                            s = step[1]
                            pe.wait_ge(x_in, 16)
                            turn_stream(step, res, s)
                            h_now[s] = step
                        elif kind == "norm_turn":
                            r, s = step[1:]
                            pe.wait_ge(normed_done, NORM_N[(r, 2 * s + 1)])
                            turn_stream(step, normed, s)
                            h_now[s] = step
                        elif kind == "ctx_turn":
                            a, s = step[1:]
                            if a == 1:
                                pe.wait_ge(ctx_masked, 2 * s + 2)
                                turn_stream(step, c_work, s)
                            elif a == 7:
                                pe.wait_ge(ctx_normed, 2 * s + 2)
                                turn_stream(step, c_work, s)
                            else:
                                pe.wait_ge(ctx_in, 16)
                                turn_stream(step, c_tok, s)
                        elif kind == "qk":
                            a, s = step[1:]
                            wait_source(a, s)
                            cols = slice(s * SW, (s + 1) * SW)
                            parts = [("q", hT), ("k", kv_of(a))]
                            if SITES[a]["rope"]:
                                parts = [("q", hT), ("qp", hT), ("k", kv_of(a)), ("kp", kv_of(a))]
                            for c in range(HP if SITES[a]["wide"] else 1):
                                for name, src in parts:
                                    job = step + (name, c)
                                    bank = ring.take(pe, job)
                                    nc.tensor.matmul(bank[:, 0:SW], W(f"w{name}{a}", c * P, P), src[:, cols],
                                                     start=True, stop=True).then_inc(ring.filled(job), 1)
                        elif kind == "v":
                            a, s = step[1:]
                            wait_source(a, s)
                            w = H * DKB // 2 if SITES[a]["wide"] else D // 2
                            if SITES[a]["wide"]:
                                for b in range(SB):
                                    job = step + (b,)
                                    bank = ring.take(pe, job)
                                    tok = kv_of(a)[:, s * SW + b * T:s * SW + (b + 1) * T]
                                    for half in range(2):
                                        i = nc.tensor.matmul(bank[half * T:(half + 1) * T, 0:w], tok,
                                                             W(f"wv{a}", half * w, w), start=True, stop=True)
                                    i.then_inc(ring.filled(job), 1)
                            else:
                                bank = ring.take(pe, step)
                                for b in range(SB):
                                    tok = kv_of(a)[:, s * SW + b * T:s * SW + (b + 1) * T]
                                    for half in range(2):
                                        i = nc.tensor.matmul(bank[half * T:(half + 1) * T, b * w:(b + 1) * w], tok,
                                                             W(f"wv{a}", half * w, w), start=True, stop=True)
                                i.then_inc(ring.filled(step), 1)
                        elif kind == "scores":
                            a, u = step[1:]
                            n = NU * a + u
                            s = u // 2
                            free = n - 1 if SITES[a]["wide"] and u > 0 else n
                            if free > 0:
                                pe.wait_ge(scores_read, free)
                            if SITES[a]["wide"]:
                                for c in range(HP):
                                    if u % 2 == 0:
                                        ring.wait_read(pe, ("qk", a, s, "q", c))
                                        ring.wait_read(pe, ("qk", a, s, "k", c))
                                    for b in range(2):
                                        bb = 2 * (u % 2) + b
                                        at = (c % 4) * P
                                        i = nc.tensor.matmul(sc[b * T:(b + 1) * T, 2 * (u % 2) + c // 4, at:at + P],
                                                             qW[:, c, bb * T:(bb + 1) * T], kW[:, c, bb, :],
                                                             start=True, stop=True)
                            else:
                                if u % 2 == 0:
                                    pe.wait_ge(k4_done, K4_N[(a, s)])
                                    if SITES[a]["rope"]:
                                        pe.wait_ge(rope_done, 2 * ROPE_N[(a, s)])
                                    else:
                                        ring.wait_read(pe, ("qk", a, s, "q", 0))
                                masked = SITES[a]["lengths"]
                                if masked:
                                    pe.wait_ge(len_masked, LEN_N[(a, s)])
                                    for b in range(2):
                                        for g in range(4):
                                            nc.tensor.matmul(sc[b * T:(b + 1) * T, g, 0:256],
                                                             own_rows[:, 2 * (u % 2) + b, :],
                                                             len_mask[:, s, g * 256:(g + 1) * 256],
                                                             start=True, stop=False, skip_group_check=True)
                                for b in range(2):
                                    tok = slice((2 * u + b) * T, (2 * u + b + 1) * T)
                                    for g in range(4):
                                        rows_ = slice(32 * g, 32 * g + 32)
                                        i = nc.tensor.matmul(sc[b * T:(b + 1) * T, g, 0:256],
                                                             qT[rows_, tok], k4[rows_, :, tok],
                                                             start=not masked, stop=True,
                                                             skip_group_check=masked)
                            i.then_inc(scores_done, 1)
                        elif kind == "lengths":
                            a, s = step[1:]
                            ring.wait_read(pe, ("qk", a, s, "k", 0))
                            pe.wait_ge(first_q_done, LEN_N[(a, s)])
                            bank = ring.take(pe, step)
                            for b in range(SB):
                                i = nc.tensor.matmul(bank[32 * b:32 * b + 32, 0:T], first_q[:, b, :],
                                                     kT[:, s * SW + b * T:s * SW + (b + 1) * T], start=True,
                                                     stop=True)
                            i.then_inc(ring.filled(step), 1)
                        elif kind == "turn":
                            a, u = step[1:]
                            pe.wait_ge(exp_done, NU * a + u + 1)
                            for half in range(2):
                                job = step + (half,)
                                bank = ring.take(pe, job)
                                for c in range(4):
                                    hp = 4 * half + c
                                    i = nc.tensor.transpose(bank[:, c * P:(c + 1) * P],
                                                            probs[:, u % 2, hp * P:(hp + 1) * P], ident)
                                i.then_inc(ring.filled(job), 1)
                        elif kind == "pv":
                            a, u = step[1:]
                            s = u // 2
                            for b in range(SB if SITES[a]["wide"] else 1):
                                ring.wait_read(pe, ("v", a, s, b) if SITES[a]["wide"] else ("v", a, s))
                            if SITES[a]["wide"]:
                                for half in range(2):
                                    ring.wait_read(pe, ("turn", a, u, half))
                                    job = step + (half,)
                                    bank = ring.take(pe, job)
                                    for c in range(4):
                                        hp = 4 * half + c
                                        for b in range(2):
                                            i = nc.tensor.matmul(bank[b * T:(b + 1) * T, c * P:(c + 1) * P],
                                                                 pT[:, u % 2, hp, b * T:(b + 1) * T],
                                                                 vW[:, 2 * (u % 2) + b, hp, :],
                                                                 start=True, stop=True)
                                    i.then_inc(ring.filled(job), 1)
                            else:
                                w = 2 * (DK + 1)
                                bank = ring.take(pe, step)
                                for half in range(2):
                                    ring.wait_read(pe, ("turn", a, u, half))
                                    for c in range(4):
                                        hp = 4 * half + c
                                        for b in range(2):
                                            i = nc.tensor.matmul(bank[b * T:(b + 1) * T, hp * w:(hp + 1) * w],
                                                                 pT[:, u % 2, hp, b * T:(b + 1) * T],
                                                                 v8[:, (2 * u + b) * HP + hp, :],
                                                                 start=True, stop=True)
                                i.then_inc(ring.filled(step), 1)
                        elif kind == "out_turn":
                            a, u = step[1:]
                            for half in range(2 if SITES[a]["wide"] else 1):
                                ring.wait_read(pe, ("pv", a, u, half) if SITES[a]["wide"] else ("pv", a, u))
                            if SITES[a]["wide"]:
                                for half in range(2):
                                    job = step + (half,)
                                    bank = ring.take(pe, job)
                                    for c in range(4):
                                        hp = 4 * half + c
                                        i = nc.tensor.transpose(bank[:, c * P:(c + 1) * P],
                                                                att[:, u % 2, hp * P:(hp + 1) * P], ident)
                                    i.then_inc(ring.filled(job), 1)
                            else:
                                bank = ring.take(pe, step + (0,))
                                nc.tensor.transpose(bank[:, 0:P], att[:, u % 2, 0:P],
                                                    ident).then_inc(ring.filled(step + (0,)), 1)
                        elif kind == "residual":
                            a, r, u = step[1:]
                            if not SITES[a]["out"]:
                                continue
                            bank = ring.take(pe, step)
                            chunks = HP if SITES[a]["wide"] else 1
                            for c in range(chunks):
                                if c % 4 == 0:
                                    ring.wait_read(pe, ("out_turn", a, u, c // 4))
                                i = nc.tensor.matmul(bank[:, 0:D], attT[:, c, :],
                                                     W(f"wo{a}", c * D, D), start=c == 0, stop=c == chunks - 1)
                            i.then_inc(ring.filled(step), 1)
                        elif kind == "ffn_up":
                            n, s = step[1:]
                            ring.wait_read(pe, h_now[s])
                            for f in range(FFN_WIDTH[n] // P):
                                job = step + (f,)
                                bank = ring.take(pe, job)
                                nc.tensor.matmul(bank[:, 0:SW], W(f"up{n}", f * P, P), hT[:, s * SW:(s + 1) * SW],
                                                 start=True, stop=True).then_inc(ring.filled(job), 1)
                        elif kind == "ffn_down":
                            n, u = step[1:]
                            nf = FFN_WIDTH[n] // P
                            bank = ring.take(pe, step)
                            for f in range(nf):
                                ring.wait_read(pe, ("ffn_up", n, u // 2, f))
                                i = nc.tensor.matmul(bank[:, 0:D], hid[:, u // 2, f, (u % 2) * P:(u % 2 + 1) * P],
                                                     W(f"down{n}", f * D, D), start=f == 0, stop=f == nf - 1)
                            i.then_inc(ring.filled(step), 1)
                        elif kind == "route":
                            u = step[1]
                            ring.wait_read(pe, h_now[u // 2])
                            bank = ring.take(pe, step)
                            nc.tensor.matmul(bank[:, 0:NE], hT[:, u * P:(u + 1) * P], W("router"), start=True,
                                             stop=True).then_inc(ring.filled(step), 1)
                        elif kind == "route_bias":
                            u = step[1]
                            pe.wait_ge(gates_done, u + 1)
                            job = ("gates_turn", u)
                            bank = ring.take(pe, job)
                            nc.tensor.transpose(bank[0:NE, 0:P], gates[:, u, :],
                                                ident).then_inc(ring.filled(job), 1)
                            ring.wait_read(pe, job)
                            bank = ring.take(pe, step)
                            nc.tensor.matmul(bank[:, 0:D], gatesT[:, u, :], expert_b[:], start=True,
                                             stop=True).then_inc(ring.filled(step), 1)
                        elif kind == "expert_up":
                            e, s = step[1:]
                            for f in range(FF // P):
                                job = step + (f,)
                                bank = ring.take(pe, job)
                                nc.tensor.matmul(bank[:, 0:SW], W(f"up_e{e}", f * P, P),
                                                 hT[:, s * SW:(s + 1) * SW], start=True,
                                                 stop=True).then_inc(ring.filled(job), 1)
                        elif kind == "expert_down":
                            e, s = step[1:]
                            for j in range(2):
                                job = step + (j,)
                                bank = ring.take(pe, job)
                                for f in range(FF // P):
                                    if j == 0:
                                        ring.wait_read(pe, ("expert_up", e, s, f))
                                    i = nc.tensor.matmul(bank[:, 0:D], hid[:, s, f, j * P:(j + 1) * P],
                                                         W(f"down_e{e}", f * D, D), start=f == 0,
                                                         stop=f == FF // P - 1)
                                i.then_inc(ring.filled(job), 1)

                @block.scalar
                def _(act):
                    steps_done = [0]

                    def link(i):
                        steps_done[0] += 1
                        i.then_inc(scalar_step, 1)
                        act.wait_ge(scalar_step, steps_done[0])

                    act.preload_act_table_set("natural_log_exp_and_others")
                    for step in steps:
                        kind = step[0]
                        if kind in ("norm", "ctx_norm"):
                            u = step[-1]
                            if kind == "norm":
                                act.wait_ge(stats_done, NORM_N[step[1:]])
                            else:
                                act.wait_ge(ctx_stats, u + 1)
                            link(nc.scalar.activation(log_var[:, u:u + 1], stat[:, u, 1:2], ACT.Ln))
                            nc.scalar.activation(rstd[:, u:u + 1], log_var[:, u:u + 1], ACT.Exp, scale=-0.5)\
                                .then_inc(rstd_done, 1)
                        if kind in ("input_turn", "norm_turn", "ctx_turn"):
                            s = step[-1]
                            bank = ring.wait_filled(act, step)
                            cols = slice(s * SW, (s + 1) * SW)
                            if kind == "input_turn" or (kind == "ctx_turn" and step[1] != 7):
                                dst = hT if kind == "input_turn" else cT
                                i = nc.scalar.activation(dst[:, cols], bank[:, 0:SW], ACT.Copy)
                            else:
                                dst, g, b = (cT, "gc", "bc") if kind == "ctx_turn" else (hT, f"g{step[1]}", f"b{step[1]}")
                                i = nc.scalar.activation(dst[:, cols], bank[:, 0:SW], ACT.Identity,
                                                         scale=COL(g), bias=COL(b))
                            i.then_inc(ring.read(step), 1)
                        elif kind == "qk" and not SITES[step[1]]["rope"]:
                            a, s = step[1:]
                            cols = slice(s * SW, (s + 1) * SW)
                            if SITES[a]["wide"]:
                                for c in range(HP):
                                    job = step + ("q", c)
                                    bank = ring.wait_filled(act, job)
                                    nc.scalar.activation(qW[:, c, :], bank[:, 0:SW], ACT.Identity,
                                                         bias=COL(f"bq{a}", c)).then_inc(ring.read(job), 1)
                            else:
                                for name, dst in (("q", qT), ("k", kT)):
                                    job = step + (name, 0)
                                    bank = ring.wait_filled(act, job)
                                    if SITES[a]["bias"]:
                                        i = nc.scalar.activation(dst[:, cols], bank[:, 0:SW], ACT.Identity,
                                                                 bias=COL(f"b{name}{a}"))
                                    else:
                                        i = nc.scalar.activation(dst[:, cols], bank[:, 0:SW], ACT.Copy)
                                    i.then_inc(ring.read(job), 1)
                        elif kind == "scores":
                            a, u = step[1:]
                            n = NU * a + u
                            if (a, u) in SHIFT_N:
                                act.wait_ge(shifted, SHIFT_N[(a, u)])
                            else:
                                act.wait_ge(scores_read, n + 1)
                            dk = DKB if SITES[a]["wide"] else DK
                            nc.scalar.activation(probs[:, u % 2, :], probs[:, u % 2, :], ACT.Exp,
                                                 scale=float(dk) ** -0.5).then_inc(exp_done, 1)
                        elif kind == "turn":
                            a, u = step[1:]
                            wait_pv(act, a, u)
                            for half in range(2):
                                bank = ring.wait_filled(act, step + (half,))
                                nc.scalar.activation(pT[:, u % 2, 4 * half:4 * half + 4, :], bank, ACT.Copy)\
                                    .then_inc(ring.read(step + (half,)), 1)
                        elif kind == "out_turn":
                            a, u = step[1:]
                            if u >= 1:
                                ring.wait_filled(act, ("residual", a, AFTER_SITE[a], u - 1))
                            for half in range(2 if SITES[a]["wide"] else 1):
                                job = step + (half,)
                                bank = ring.wait_filled(act, job)
                                w = 4 if SITES[a]["wide"] else 1
                                nc.scalar.activation(attT[:, 4 * half:4 * half + w, :],
                                                     bank[:, 0:w * P], ACT.Copy).then_inc(ring.read(job), 1)
                        elif kind in ("ffn_up", "expert_up"):
                            n, s = step[1:]
                            width = FFN_WIDTH[n] if kind == "ffn_up" else FF
                            if kind == "expert_up":
                                fn, bias = ACT.Gelu, f"up_be{n}"
                                if n > 0:
                                    ring.wait_filled(act, ("expert_down", n - 1, s, 1))
                            else:
                                fn, bias = (ACT.Gelu_apprx_tanh if n == 2 else ACT.Relu), f"up_b{n}"
                            for f in range(width // P):
                                job = step + (f,)
                                bank = ring.wait_filled(act, job)
                                nc.scalar.activation(hid[:, s, f, :], bank[:, 0:SW], fn,
                                                     bias=COL(bias, f)).then_inc(ring.read(job), 1)
                            if step == ("ffn_up", 2, NS - 1):
                                act.preload_act_table_set("natural_log_exp_and_others")
                        elif kind == "route":
                            u = step[1]
                            act.wait_ge(route_diff, u + 1)
                            nc.scalar.activation(share[:, u, 1:2], share[:, u, 0:1], ACT.Exp).then_inc(route_exp, 1)
                        elif kind == "route_bias":
                            u = step[1]
                            job = ("gates_turn", u)
                            bank = ring.wait_filled(act, job)
                            nc.scalar.activation(gatesT[:, u, :], bank[0:NE, 0:P], ACT.Copy)\
                                .then_inc(ring.read(job), 1)

                @block.vector
                def _(dve):
                    steps_done = [0]

                    def link(i):
                        steps_done[0] += 1
                        i.then_inc(vector_step, 1)
                        dve.wait_ge(vector_step, steps_done[0])

                    def refine(u, n):
                        dve.wait_ge(rstd_done, n)
                        r1 = rstd[:, u:u + 1]
                        link(nc.vector.tensor_scalar(newton[:, 0:1], stat[:, u, 1:2], r1, r1, ALU.mult, ALU.mult))
                        link(nc.vector.tensor_scalar(newton[:, 0:1], newton[:, 0:1], -0.5, 1.5, ALU.mult, ALU.add))
                        link(nc.vector.tensor_scalar(newton[:, 1:2], newton[:, 0:1], r1, None, ALU.mult))

                    def heads(ap, k=T):
                        return ap.rearrange("p (h k) -> p h k", k=k)

                    def over_keys(ap):
                        return ap.rearrange("p (h o) -> p h o", o=1).to_broadcast([P, H, T])

                    for step in steps:
                        kind = step[0]
                        if kind == "masks":
                            dve.wait_ge(x_in, 16)
                            for u in range(NU):
                                link(nc.vector.tensor_reduce(top[:, 0:1], res[:, u, :], X_AXIS, ALU.max,
                                                             apply_absolute_value=True))
                                link(nc.vector.tensor_scalar(tok_mask[:, 0, u:u + 1], top[:, 0:1], 0.0, None,
                                                             ALU.is_gt))
                            dve.wait_ge(mask_in, 16 * NB)
                            link(nc.vector.tensor_scalar(pad[:], mask_u8[:], -1.0, BIG, ALU.add, ALU.mult))
                            for u in range(NU):
                                link(nc.vector.tensor_tensor(pad_causal[:, u, :], pad[:, u, :], K("causal"), ALU.add))
                        elif kind == "qk":
                            a, s = step[1:]
                            cols = slice(s * SW, (s + 1) * SW)
                            if SITES[a]["wide"]:
                                for c in range(HP):
                                    job = step + ("k", c)
                                    bank = ring.wait_filled(dve, job)
                                    for half in range(2):
                                        ps = slice(half * T, (half + 1) * T)
                                        i = nc.vector.tensor_scalar(
                                            kW[ps, c, :, ps], bank[ps, 0:SW].rearrange("p (b t) -> p b t", t=T),
                                            COL(f"bk{a}", c)[ps], None, ALU.add)
                                    i.then_inc(ring.read(job), 1)
                                continue
                            if SITES[a]["rope"]:
                                n = ROPE_N[(a, s)]
                                for k, name in enumerate(("q", "k")):
                                    if n > 1:
                                        dve.wait_ge(rope_done, 2 * (n - 1) - 1 + k)
                                    for part, table, buf in ((name, "cos", rope_a), (name + "p", "sin", rope_b)):
                                        job = step + (part, 0)
                                        bank = ring.wait_filled(dve, job)
                                        nc.vector.scalar_tensor_tensor(
                                            buf[:, k, :], bank[:, 0:SW], COL(f"b{part}{a}"), K(table),
                                            ALU.add, ALU.mult).then_inc(ring.read(job), 1)
                                dve.wait_ge(rope_done, 2 * n)
                            else:
                                ring.wait_read(dve, step + ("k", 0))
                            for j in range(4):
                                i = nc.vector.tensor_scalar(k4[:, j, cols], kT[:, cols], K("head_of_four", j, 1), None,
                                                            ALU.mult)
                            i.then_inc(k4_done, 1)
                        elif kind == "lengths":
                            a, s = step[1:]
                            ring.wait_read(dve, ("qk", a, s, "q", 0))
                            q0 = qT[:, s * SW:(s + 1) * SW:T].rearrange("p (b o) -> p b o", o=1)
                            nc.vector.tensor_tensor(
                                first_q[:], K("head_of_all").rearrange("p (o h) -> p o h", o=1).to_broadcast([P, SB, 32]),
                                q0.to_broadcast([P, SB, 32]), ALU.mult).then_inc(first_q_done, 1)
                            bank = ring.wait_filled(dve, step)
                            nc.vector.tensor_scalar(flags[:], bank[:, 0:T], 0.0, None, ALU.not_equal)\
                                .then_inc(ring.read(step), 1)
                            ring.wait_read(dve, step)
                            link(nc.vector.tensor_reduce(count[:], flags[:], X_AXIS, ALU.add))
                            nc.vector.tensor_scalar(late[:], K("iota"), count[:], -BIG, ALU.is_ge, ALU.mult)\
                                .then_inc(counted, 1)
                        elif kind == "v":
                            a, s = step[1:]
                            if SITES[a]["wide"]:
                                w = H * DKB // 2
                                for b in range(SB):
                                    job = step + (b,)
                                    bank = ring.wait_filled(dve, job)
                                    for half in range(2):
                                        ps = slice(half * T, (half + 1) * T)
                                        i = nc.vector.tensor_tensor(
                                            vW[ps, b, :, ps], bank[ps, 0:w].rearrange("p (h d) -> p h d", d=DKB),
                                            ROW(f"bv{a}", half * w, w)[ps].rearrange("p (h d) -> p h d", d=DKB),
                                            ALU.add)
                                    i.then_inc(ring.read(job), 1)
                            else:
                                bank = ring.wait_filled(dve, step)
                                w = D // 2
                                for half in range(2):
                                    ps = slice(half * T, (half + 1) * T)
                                    lo = half * (DK + 1)
                                    dst = v8[ps, s * SB * HP:(s + 1) * SB * HP, lo:lo + DK]
                                    src = bank[ps, 0:SB * w].rearrange("p (h d) -> p h d", d=DK)
                                    if SITES[a]["bias"]:
                                        dst = dst.rearrange("p (b h) d -> p b h d", b=SB)
                                        src = src.rearrange("p (b h) d -> p b h d", b=SB)
                                        bias = ROW(f"bv{a}", half * w, w)[ps].rearrange("p (o h d) -> p o h d", o=1, d=DK)
                                        i = nc.vector.tensor_tensor(dst, src, bias.to_broadcast([T, SB, HP, DK]),
                                                                    ALU.add)
                                    else:
                                        i = nc.vector.tensor_copy(dst, src)
                                i.then_inc(ring.read(step), 1)
                        elif kind == "scores":
                            a, u = step[1:]
                            n = NU * a + u
                            if SITES[a]["wide"]:
                                S = sc[:, 2 * (u % 2):2 * (u % 2) + 2, :]
                            else:
                                S = sc[:, :, 0:256]
                            banks = S.shape[1]
                            S4 = S.rearrange("p g (j k) -> p g j k", k=T)
                            pr = probs[:, u % 2, :]
                            pr3 = pr.rearrange("p (g w) -> p g w", g=banks)
                            pr4 = pr.rearrange("p (g j k) -> p g j k", g=banks, k=T)
                            dve.wait_ge(scores_done, n + 1)
                            if n >= 2:
                                m = n - 2
                                ring.wait_filled(dve, ("turn", m // NU, m % NU, 1))
                            if SITES[a]["wide"] or SITES[a]["causal"]:
                                if SITES[a]["wide"]:
                                    m_ap = (pad_causal if SITES[a]["causal"] else pad)[:, u, :]
                                else:
                                    m_ap = K("causal")
                                m_ap = m_ap.rearrange("p (a o k) -> p a o k", a=1, o=1)
                                nc.vector.tensor_tensor(pr4, S4, m_ap.to_broadcast([P, banks, H // banks, T]),
                                                        ALU.add).then_inc(scores_read, 1)
                                dve.wait_ge(scores_read, n + 1)
                                from_ = heads(pr)
                            else:
                                from_ = None
                            if from_ is None:
                                link(nc.vector.tensor_reduce(top[:].rearrange("p (g j) -> p g j", g=4), S4, X_AXIS,
                                                             ALU.max))
                                top4 = top[:].rearrange("p (g j o) -> p g j o", g=4, o=1)
                                nc.vector.tensor_tensor(pr4, S4, top4.to_broadcast([P, 4, 4, T]), ALU.subtract)\
                                    .then_inc(scores_read, 1)
                            else:
                                link(nc.vector.tensor_reduce(top[:], from_, X_AXIS, ALU.max))
                                nc.vector.tensor_tensor(from_, from_, over_keys(top[:]), ALU.subtract)\
                                    .then_inc(shifted, 1)
                                dve.wait_ge(shifted, SHIFT_N[(a, u)])
                        elif kind == "turn":
                            a, u = step[1:]
                            n = NU * a + u
                            if SITES[a]["wide"]:
                                dve.wait_ge(exp_done, n + 1)
                                link(nc.vector.tensor_reduce(den[:], heads(probs[:, u % 2, :]), X_AXIS, ALU.add))
                        elif kind == "pv":
                            a, u = step[1:]
                            n = NU * a + u
                            if SITES[a]["wide"]:
                                mask_t = (pad_causal if SITES[a]["causal"] else pad)[:, u, :]
                                link(nc.vector.tensor_reduce(valid[:, 0:1], mask_t, X_AXIS, ALU.max))
                                link(nc.vector.tensor_scalar(valid[:, 1:2], valid[:, 0:1], -BIG / 2, None, ALU.is_gt))
                                link(nc.vector.reciprocal(den[:], den[:]))
                                link(nc.vector.tensor_scalar(den[:], den[:], valid[:, 1:2], None, ALU.mult))
                                if OUT_N[(a, u)] > 2:
                                    wait_att(dve, a, u)
                                for half in range(2):
                                    job = step + (half,)
                                    bank = ring.wait_filled(dve, job)
                                    r8 = den[:, 8 * half:8 * half + 8].rearrange("p (h o) -> p h o", o=1)
                                    nc.vector.tensor_tensor(
                                        att[:, u % 2, 512 * half:512 * half + 512].rearrange("p (h d) -> p h d", d=DKB),
                                        bank.rearrange("p (h d) -> p h d", d=DKB), r8.to_broadcast([P, 8, DKB]),
                                        ALU.mult).then_inc(ring.read(job), 1)
                                ring.wait_read(dve, job)
                            else:
                                bank = ring.wait_filled(dve, step)
                                o9 = bank[:, 0:H * (DK + 1)].rearrange("p (h d) -> p h d", d=DK + 1)
                                link(nc.vector.reciprocal(den[:].rearrange("p (h o) -> p h o", o=1), o9[:, :, DK:DK + 1]))
                                if SITES[a]["lengths"]:
                                    if a == 1:
                                        dve.wait_ge(tok_masked, u + 1)
                                    link(nc.vector.tensor_scalar(den[:], den[:], tok_mask[:, a, u:u + 1], None,
                                                                 ALU.mult))
                                dst = scaled[:, u % 2, :] if SITES[a]["lengths"] else att[:, u % 2, 0:P]
                                if not SITES[a]["lengths"] and OUT_N[(a, u)] > 2:
                                    wait_att(dve, a, u)
                                r8 = den[:].rearrange("p (h o) -> p h o", o=1).to_broadcast([P, H, DK])
                                nc.vector.tensor_tensor(dst.rearrange("p (h d) -> p h d", d=DK), o9[:, :, 0:DK], r8,
                                                        ALU.mult).then_inc(ring.read(step), 1)
                                ring.wait_read(dve, step)
                        elif kind == "residual":
                            a, r, u = step[1:]
                            if r == 0:
                                dve.wait_ge(x_in, 16)
                            else:
                                dve.wait_ge(res_done, NORM_N[(r - 1, u)])
                            if SITES[a]["out"]:
                                bank = ring.wait_filled(dve, step)
                                nc.vector.tensor_tensor(raw[:, u, :], bank[:, 0:D], res[:, u, :], ALU.add)\
                                    .then_inc(ring.read(step), 1)
                                ring.wait_read(dve, step)
                            else:
                                link(nc.vector.tensor_tensor(raw[:, u, :], scaled[:, u % 2, :], res[:, u, :], ALU.add))
                        elif kind == "ffn_down":
                            n, u = step[1:]
                            r = AFTER_FFN[n]
                            dve.wait_ge(res_done, NORM_N[(r - 1, u)])
                            bank = ring.wait_filled(dve, step)
                            if n == 0:
                                nc.vector.tensor_tensor(scaled[:, u % 2, :], bank[:, 0:D], ROW("down_b0"), ALU.add)\
                                    .then_inc(ring.read(step), 1)
                                ring.wait_read(dve, step)
                                link(nc.vector.scalar_tensor_tensor(raw[:, u, :], scaled[:, u % 2, :],
                                                                    tok_mask[:, 0, u:u + 1], res[:, u, :], ALU.mult,
                                                                    ALU.add))
                            else:
                                nc.vector.tensor_tensor(raw[:, u, :], bank[:, 0:D], res[:, u, :], ALU.add)\
                                    .then_inc(ring.read(step), 1)
                                ring.wait_read(dve, step)
                        elif kind == "norm":
                            r, u = step[1:]
                            src = raw
                            if r == LN_ONLY:
                                dve.wait_ge(res_done, NORM_N[(r - 1, u)])
                                src = res
                            link(nc.vector.bn_stats(stat6[:], src[:, u, :]))
                            link(nc.vector.bn_aggr(stat[:, u, :], stat6[:]))
                            nc.vector.tensor_scalar(stat[:, u, 1:2], stat[:, u, 1:2], NORMS[r]["eps"], None,
                                                    ALU.add).then_inc(stats_done, 1)
                            refine(u, RSTD_N[step])
                            nc.vector.tensor_scalar(normed[:, u, :], src[:, u, :], stat[:, u, 0:1], newton[:, 1:2],
                                                    ALU.subtract, ALU.mult).then_inc(normed_done, 1)
                            dve.wait_ge(normed_done, NORM_N[(r, u)])
                        elif kind == "ctx_mask":
                            u = step[1]
                            dve.wait_ge(res_done, NORM_N[(0, u)])
                            link(nc.vector.tensor_reduce(top[:, 0:1], res[:, u, :], X_AXIS, ALU.max,
                                                         apply_absolute_value=True))
                            nc.vector.tensor_scalar(tok_mask[:, 1, u:u + 1], top[:, 0:1], 0.0, None, ALU.is_gt)\
                                .then_inc(tok_masked, 1)
                            dve.wait_ge(tok_masked, u + 1)
                        elif kind == "ctx_norm":
                            u = step[1]
                            link(nc.vector.bn_stats(stat6[:], c_tok[:, u, :]))
                            link(nc.vector.bn_aggr(stat[:, u, :], stat6[:]))
                            nc.vector.tensor_scalar(stat[:, u, 1:2], stat[:, u, 1:2], CTX_NORM["eps"], None,
                                                    ALU.add).then_inc(ctx_stats, 1)
                            refine(u, RSTD_N[step])
                            nc.vector.tensor_scalar(c_work[:, u, :], c_tok[:, u, :], stat[:, u, 0:1], newton[:, 1:2],
                                                    ALU.subtract, ALU.mult).then_inc(ctx_normed, 1)
                            dve.wait_ge(ctx_normed, u + 1)
                        elif kind == "route":
                            u = step[1]
                            bank = ring.wait_filled(dve, step)
                            nc.vector.tensor_tensor(logits[:, u, :], bank[:, 0:NE], ROW("router_b"), ALU.add)\
                                .then_inc(ring.read(step), 1)
                            ring.wait_read(dve, step)
                            link(nc.vector.max(best[:, u, :], logits[:, u, :]))
                            link(nc.vector.max_index(best_i[:, u, :], best[:, u, :], logits[:, u, :]))
                            nc.vector.tensor_tensor(share[:, u, 0:1], best[:, u, 1:2], best[:, u, 0:1],
                                                    ALU.subtract).then_inc(route_diff, 1)
                        elif kind == "route_bias":
                            u = step[1]
                            dve.wait_ge(route_exp, u + 1)
                            link(nc.vector.tensor_scalar(share[:, u, 2:3], share[:, u, 1:2], 1.0, None, ALU.add))
                            link(nc.vector.reciprocal(share[:, u, 2:3], share[:, u, 2:3]))
                            link(nc.vector.tensor_tensor(share[:, u, 3:4], share[:, u, 1:2], share[:, u, 2:3],
                                                         ALU.mult))
                            link(nc.vector.tensor_copy(best_f[:], best_i[:, u, :]))
                            for k in range(2):
                                link(nc.vector.tensor_scalar(one_hot[:, k, :], K("iota", 0, NE), best_f[:, k:k + 1],
                                                             share[:, u, 2 + k:3 + k], ALU.is_equal, ALU.mult))
                            nc.vector.tensor_tensor(gates[:, u, :], one_hot[:, 0, :], one_hot[:, 1, :], ALU.add)\
                                .then_inc(gates_done, 1)
                            dve.wait_ge(gates_done, u + 1)
                            bank = ring.wait_filled(dve, step)
                            nc.vector.tensor_tensor(raw[:, u, :], bank[:, 0:D], raw[:, u, :], ALU.add)\
                                .then_inc(ring.read(step), 1)
                            ring.wait_read(dve, step)
                        elif kind == "expert_down":
                            e, s = step[1:]
                            for j in range(2):
                                u = 2 * s + j
                                job = step + (j,)
                                bank = ring.wait_filled(dve, job)
                                nc.vector.scalar_tensor_tensor(raw[:, u, :], bank[:, 0:D], gates[:, u, e:e + 1],
                                                               raw[:, u, :], ALU.mult, ALU.add)\
                                    .then_inc(ring.read(job), 1)
                                ring.wait_read(dve, job)

                @block.gpsimd
                def _(pool):
                    steps_done = [0]

                    def link(i):
                        steps_done[0] += 1
                        i.then_inc(pool_step, 1)
                        pool.wait_ge(pool_step, steps_done[0])

                    for step in steps:
                        kind = step[0]
                        if kind == "lengths":
                            a, s = step[1:]
                            pool.wait_ge(counted, LEN_N[(a, s)])
                            nc.gpsimd.tensor_tensor(
                                len_mask[:, s, :].rearrange("p (h k) -> p h k", k=T),
                                K("own_head").rearrange("p (h o) -> p h o", o=1).to_broadcast([P, H, T]),
                                late[:].rearrange("p (o k) -> p o k", o=1).to_broadcast([P, H, T]), ALU.mult)\
                                .then_inc(len_masked, 1)
                        elif kind == "norm":
                            r, u = step[1:]
                            norm = NORMS[r]
                            src = res if r == LN_ONLY else raw
                            pool.wait_ge(normed_done, NORM_N[(r, u)])
                            if norm["post"]:
                                link(nc.gpsimd.tensor_tensor(res[:, u, :], normed[:, u, :], ROW(f"g{r}"), ALU.mult))
                                i = nc.gpsimd.tensor_tensor(res[:, u, :], res[:, u, :], ROW(f"b{r}"), ALU.add)
                                if norm["add"]:
                                    link(i)
                                    i = nc.gpsimd.tensor_tensor(res[:, u, :], res[:, u, :], ROW(f"add{r}"), ALU.add)
                            elif norm["add"]:
                                i = nc.gpsimd.tensor_tensor(res[:, u, :], src[:, u, :], ROW(f"add{r}"), ALU.add)
                            if norm["post"] or norm["add"]:
                                i.then_inc(res_done, 1)
                        elif kind == "ctx_mask":
                            u = step[1]
                            if u == 0:
                                pool.wait_ge(ctx_in, 16)
                            pool.wait_ge(tok_masked, u + 1)
                            nc.gpsimd.tensor_scalar(c_work[:, u, :], c_tok[:, u, :], tok_mask[:, 1, u:u + 1], None,
                                                    ALU.mult).then_inc(ctx_masked, 1)
                        elif kind == "qk" and SITES[step[1]]["rope"]:
                            a, s = step[1:]
                            n = ROPE_N[(a, s)]
                            cols = slice(s * SW, (s + 1) * SW)
                            for k, (name, dst) in enumerate((("q", qT), ("k", kT))):
                                ring.wait_read(pool, step + (name, 0))
                                ring.wait_read(pool, step + (name + "p", 0))
                                nc.gpsimd.tensor_tensor(dst[:, cols], rope_a[:, k, :], rope_b[:, k, :], ALU.add)\
                                    .then_inc(rope_done, 1)

                @block.sync
                def _(sp):
                    sp.dma_start(res[:], x[tile].rearrange("u p d -> p u d")).then_inc(x_in, 16)
                    for b in range(NB):
                        sp.dma_start(mask_u8[(b % 2) * T:(b % 2 + 1) * T, b // 2, :],
                                     mask[tile][b:b + 1, :].to_broadcast([T, T])).then_inc(mask_in, 16)
                    sp.dma_start(c_tok[:], ctx[tile].rearrange("u p d -> p u d")).then_inc(ctx_in, 16)
                    for u in range(NU):
                        ring.wait_read(sp, ("expert_down", NE - 1, u // 2, u % 2))
                    sp.dma_start(out[tile].rearrange("u p d -> p u d"), raw[:]).then_inc(out_stored, 16)
                    sp.wait_ge(out_stored, 16)

            with nc.Block() as block:
                @block.sync
                def _(sp):
                    for s in per_tile:
                        sp.sem_clear(s)


def _halves(w, heads, dk):
    w = w.reshape(w.shape[0], heads, dk)
    return np.concatenate([w[:, 0::2].reshape(w.shape[0], -1), w[:, 1::2].reshape(w.shape[0], -1)], axis=1)


def _rotated(w):
    w = w.reshape(w.shape[0], H, 2, DK // 2)
    return w[:, :, ::-1].reshape(w.shape[0], -1)


def _by_rows(w):
    n = w.shape[0] // P
    return w.reshape(n, P, w.shape[1]).transpose(1, 0, 2).reshape(P, -1)


def lay_out(t):
    wq, cols, rows = {}, {}, {}
    for r, norm in enumerate(NORMS):
        cols[f"g{r}"], cols[f"b{r}"] = t[norm["g"]][:, None], t[norm["b"]][:, None]
        if norm["post"]:
            rows[f"g{r}"], rows[f"b{r}"] = t[norm["g"]], t[norm["b"]]
        if norm["add"]:
            rows[f"add{r}"] = t[norm["add"]]
    cols["gc"], cols["bc"] = t[CTX_NORM["g"]][:, None], t[CTX_NORM["b"]][:, None]
    for a, site in enumerate(SITES):
        layer = site["layer"]
        if layer == 0:
            n = 2 if site["cross"] else 1
            w = {k: t[f"L0_xattn_W{k}{n}"].transpose(1, 0, 2).reshape(D, D) for k in "qkv"}
            b = {}
        elif layer in (1, 2):
            pre = f"L{layer}_xattn_{'ca' if site['cross'] else 'sa'}_"
            w = {k: t[f"{pre}w{k}"] for k in "qkvo"}
            b = {k: t[f"{pre}b{k}"] for k in "qkv"}
        else:
            pre = f"L3_xattn_{'ca' if site['cross'] else 'sa'}_"
            w = {k: t[pre + "in_w"][n * D:(n + 1) * D].T for n, k in enumerate("qkv")}
            w["o"] = t[pre + "out_w"].T
            b = {k: t[pre + "in_b"][n * D:(n + 1) * D] for n, k in enumerate("qkv")}
        dk = DKB if site["wide"] else DK
        wq[f"wq{a}"], wq[f"wk{a}"] = w["q"], w["k"]
        wq[f"wv{a}"] = _halves(w["v"], H, dk)
        if site["rope"]:
            wq[f"wqp{a}"], wq[f"wkp{a}"] = _rotated(w["q"]), _rotated(w["k"])
            cols[f"bqp{a}"], cols[f"bkp{a}"] = _rotated(b["q"][None]).T, _rotated(b["k"][None]).T
        if site["out"]:
            wq[f"wo{a}"] = _by_rows(w["o"])
        if site["bias"]:
            cols[f"bq{a}"], cols[f"bk{a}"] = b["q"].reshape(-1, P).T, b["k"].reshape(-1, P).T
            rows[f"bv{a}"] = _halves(b["v"][None], H, dk)[0]
    up = {0: t["L0_xattn_fc1_w"].T, 1: t["L1_xattn_ffn_w1"], 2: t["L2_xattn_fc1_w"]}
    down = {0: t["L0_xattn_fc2_w"].T, 1: t["L1_xattn_ffn_w2"], 2: t["L2_xattn_fc2_w"]}
    up_b = {0: t["L0_xattn_fc1_b"], 1: t["L1_xattn_ffn_b1"], 2: t["L2_xattn_fc1_b"]}
    for n in FFN_WIDTH:
        wq[f"up{n}"], wq[f"down{n}"] = up[n], _by_rows(down[n])
        cols[f"up_b{n}"] = up_b[n].reshape(-1, P).T
    wq["router"] = t["L3_xattn_router_w"].T
    for e in range(NE):
        wq[f"up_e{e}"] = t["L3_xattn_e_fc1_w"][e].T
        wq[f"down_e{e}"] = _by_rows(t["L3_xattn_e_fc2_w"][e].T)
        cols[f"up_be{e}"] = t["L3_xattn_e_fc1_b"][e].reshape(-1, P).T
    rows["down_b0"] = t["L0_xattn_fc2_b"]
    rows["router_b"] = t["L3_xattn_router_b"]
    weights = np.concatenate([wq[k] for k in W_AT], axis=1)
    columns = np.concatenate([cols[k] for k in C_AT], axis=1)
    row = np.concatenate([rows[k] for k in R_AT])[None]
    return weights, columns, row


def shape_constants():
    c = {}
    part = np.arange(P)
    c["ident"] = np.eye(P)
    c["head_of_four"] = (part[:, None] // DK % 4 == np.arange(4)[None]).astype(np.float32)
    c["causal"] = np.where(np.arange(T)[None] > (part % T)[:, None], -4 * BIG, 0.0)
    c["iota"] = np.broadcast_to(np.arange(T), (P, T))
    c["head_of_all"] = (part[:, None] // DK == np.arange(32)[None]).astype(np.float32)
    c["own_head"] = (part[:, None] % 32 == np.arange(H)[None]).astype(np.float32)
    c["own_rows"] = (part[:, None] // 32 == np.arange(SB)[None]).astype(np.float32)
    inv = (1.0 / np.float32(10000.0) ** (np.arange(0, DK, 2, dtype=np.float32) / np.float32(DK))).astype(np.float32)
    angle = np.outer(np.arange(T, dtype=np.float32), inv).astype(np.float32)
    cos, sin = np.cos(angle), np.sin(angle)
    d = part % DK
    sign = np.where(d < DK // 2, -1.0, 1.0)[:, None]
    c["cos"] = np.tile(cos.T[d % (DK // 2)], (1, SW // T))
    c["sin"] = np.tile(sin.T[d % (DK // 2)] * sign, (1, SW // T))
    return np.ascontiguousarray(np.concatenate([c[k] for k in K_AT], axis=1).astype(np.float32))


def kernel(**inputs):
    import concourse.bacc as bacc
    from concourse.bass_utils import run_bass_kernel_spmd

    t = {k: np.asarray(v) for k, v in inputs.items()}
    weights, columns, rows = lay_out(t)
    arrays = {
        "x": t["x"].reshape(ITERS, NU, P, D),
        "ctx": t["ctx_1024"].reshape(ITERS, NU, P, D),
        "mask": t["mask_BxS2_bf1"].view(np.uint8).reshape(ITERS, NB, T),
        "weights": weights,
        "columns": columns,
        "rows": rows,
        "constants": shape_constants(),
        "expert_bias": t["L3_xattn_e_fc2_b"],
    }
    arrays = {k: np.ascontiguousarray(v) for k, v in arrays.items()}
    nc = bacc.Bacc("TRN2", target_bir_lowering=False, num_devices=1)
    args = [nc.dram_tensor(k, a.shape, mybir.dt.from_np(a.dtype), kind="ExternalInput").ap() for k, a in arrays.items()]
    out = nc.dram_tensor("out", (ITERS, NU, P, D), F32, kind="ExternalOutput").ap()
    decoder_stack(nc, *args, out)
    r = run_bass_kernel_spmd(nc, [arrays], core_ids=[0])
    return r.results[0]["out"].reshape(B, T, D)
```

```python
from contextlib import ExitStack

import numpy as np

from concourse import mybir

P = 128
B, T, D, H = 128, 64, 128, 16
NU = 4
NS = NU // 2
TOK = NU * P
ITERS = B * T // TOK
NB = TOK // T
SB = NB // NS
SW = TOK // NS
HP = H // 2
DK = D // H
DKB = 64
FF = 512
NE = 8
BIG = 1.0e30
EPS_SMALL, EPS_LARGE = 1e-12, 1e-5
F32 = mybir.dt.float32
BF16 = mybir.dt.bfloat16
U8 = mybir.dt.uint8
U32 = mybir.dt.uint32
ALU = mybir.AluOpType
ACT = mybir.ActivationFunctionType
X_AXIS = mybir.AxisListType.X

SITES = [
    dict(layer=0, cross=False, causal=True, wide=False, rope=False, lengths=True, bias=False, out=False),
    dict(layer=0, cross=True, causal=False, wide=False, rope=False, lengths=True, bias=False, out=False),
    dict(layer=1, cross=False, causal=True, wide=True, rope=False, lengths=False, bias=True, out=True),
    dict(layer=1, cross=True, causal=False, wide=True, rope=False, lengths=False, bias=True, out=True),
    dict(layer=2, cross=False, causal=True, wide=False, rope=True, lengths=False, bias=True, out=True),
    dict(layer=2, cross=True, causal=False, wide=False, rope=True, lengths=False, bias=True, out=True),
    dict(layer=3, cross=False, causal=False, wide=False, rope=False, lengths=False, bias=True, out=True),
    dict(layer=3, cross=True, causal=False, wide=False, rope=False, lengths=False, bias=True, out=True),
]

NORMS = [
    dict(g="L0_xattn_ln1_g", b="L0_xattn_ln1_b", eps=EPS_LARGE, post=True, add=None),
    dict(g="L0_xattn_ln2_g", b="L0_xattn_ln2_b", eps=EPS_LARGE, post=True, add=None),
    dict(g="L0_xattn_ln3_g", b="L0_xattn_ln3_b", eps=EPS_LARGE, post=True, add="L1_xattn_sa_bo"),
    dict(g="L1_xattn_ln1_g", b="L1_xattn_ln1_b", eps=EPS_SMALL, post=True, add="L1_xattn_ca_bo"),
    dict(g="L1_xattn_ln2_g", b="L1_xattn_ln2_b", eps=EPS_SMALL, post=True, add="L1_xattn_ffn_b2"),
    dict(g="L1_xattn_ln3_g", b="L1_xattn_ln3_b", eps=EPS_SMALL, post=True, add=None),
    dict(g="L2_xattn_ln1_g", b="L2_xattn_ln1_b", eps=EPS_LARGE, post=False, add="L2_xattn_sa_bo"),
    dict(g="L2_xattn_ln2_g", b="L2_xattn_ln2_b", eps=EPS_LARGE, post=False, add="L2_xattn_ca_bo"),
    dict(g="L2_xattn_ln3_g", b="L2_xattn_ln3_b", eps=EPS_LARGE, post=False, add="L2_xattn_fc2_b"),
    dict(g="L3_xattn_sa_ln_g", b="L3_xattn_sa_ln_b", eps=EPS_LARGE, post=False, add="L3_xattn_sa_out_b"),
    dict(g="L3_xattn_ca_q_ln_g", b="L3_xattn_ca_q_ln_b", eps=EPS_LARGE, post=False, add="L3_xattn_ca_out_b"),
    dict(g="L3_xattn_moe_ln_g", b="L3_xattn_moe_ln_b", eps=EPS_LARGE, post=False, add=None),
]
CTX_NORM = dict(g="L3_xattn_ca_kv_ln_g", b="L3_xattn_ca_kv_ln_b", eps=EPS_LARGE)
AFTER_SITE = {0: 0, 1: 1, 2: 3, 3: 4, 4: 7, 5: 8, 6: 10, 7: 11}
AFTER_FFN = {0: 2, 1: 5, 2: 9}
LN_ONLY = 6
CTX_TURNS = (1, 3, 7)
FFN_WIDTH = {0: D, 1: FF, 2: FF}


ORDER = {
    "site0": """old_sums old_pv old_scale warm1 ctx_turn0 k0 old_probs_turn q0 warm5 lengths0
        old_residual old_out_turn v0 old_add old_last old_rstd old_norm warm17 scores0 warm11 ctx_turn1
        warm1 k1 old_turn warm4 q1 warm23 scores1 exp0 shift0 lengths1 turn0 shift1 v1 exp1 warm13
        scores2 shift2 exp2 pv0 turn1 warm1 scores3 scale0 add0 exp3 shift3 scale1 turn2 add1 rstd0 pv1
        pv2 norm0 scale2 turn3 add2 norm_turn0 pv3 scale3 warm3""",
    "site1": """old_sums old_pv old_scale ctx_turn0 warm1 k0 old_probs_turn q0 warm5 lengths0
        old_residual old_out_turn v0 old_add old_last old_rstd old_norm warm17 scores0 warm12 ctx_turn1
        k1 old_turn warm4 q1 warm23 scores1 exp0 shift0 lengths1 turn0 shift1 v1 exp1 warm13 scores2
        shift2 exp2 pv0 turn1 warm1 scores3 scale0 add0 exp3 shift3 scale1 turn2 add1 rstd0 pv1 warm9
        pv2 norm0 turn3 scale2 add2 norm_turn0 warm3 pv3""",
    "ffn0": """old_probs_turn old_residual warm2 old_sums old_pv old_scale warm1 up0 old_rstd old_last
        old_out_turn old_add old_norm warm29 old_turn down0 down1 warm8 up1 rstd0 norm0 warm28
        norm_turn0 down2""",
    "site2": """ctx_turn0 old_pv qk0 old_probs_turn old_scale old_sums old_last old_out_turn
        old_residual old_add old_norm scores0 old_rstd shift0 scores1 exp0 v0 warm2 old_turn shift1
        ctx_turn1 warm1 turn0 exp1 sums0 warm15 qk1 turn1 sums1 exp2 pv0 scale0 scores2 shift2 pv1
        scale1 warm4 v1 scores3 out_turn0 warm1 residual0 shift3 out_turn1 warm5 turn2 exp3 add0 sums2
        residual1 add1 pv2 scale2 rstd0 norm0 turn3 sums3 warm1 pv3 scale3 out_turn2 add2 norm_turn0
        warm1 residual2""",
    "site3": """ctx_turn0 old_probs_turn old_sums old_pv old_scale qk0 old_last old_out_turn
        old_residual old_add old_norm scores0 old_rstd shift0 scores1 v0 warm2 exp0 old_turn shift1
        ctx_turn1 warm3 turn0 exp1 sums0 warm15 qk1 turn1 sums1 exp2 pv0 scale0 scores2 shift2 pv1
        scale1 warm4 v1 scores3 out_turn0 warm3 residual0 shift3 out_turn1 warm5 turn2 residual1 exp3
        add0 sums2 add1 scale2 pv2 rstd0 norm0 turn3 sums3 warm2 pv3 scale3 out_turn2 add2 norm_turn0
        residual2""",
    "ffn1": """old_pv old_sums old_out_turn old_scale up0 old_last warm5 old_residual old_probs_turn
        old_add old_rstd warm22 old_turn old_norm down0 down1 up1 rstd0 norm0 warm8 stats0 again_rstd0
        stats1 again_norm0 down2 warm38 norm_turn0""",
    "site4": """old_scale old_sums old_pv old_last old_out_turn old_rstd old_probs_turn warm1
        old_residual old_add q0 v0 k0 old_norm warm22 scores0 warm18 old_turn warm4 exp0 shift0 k1 q1 v1
        scores1 turn0 shift1 warm17 scores2 pv0 shift2 warm4 exp1 exp2 turn1 warm1 scale0 out_turn0
        warm11 residual0 add0 warm2 scores3 pv1 shift3 exp3 warm2 scale1 turn2 warm3 out_turn1 warm3
        residual1 rstd0 add1 norm0 scale2 warm4 pv2 turn3 warm5 out_turn2 warm2 residual2 add2 warm1 pv3
        scale3 norm_turn0""",
    "site5": """old_scale old_sums old_pv old_last old_out_turn old_rstd old_probs_turn warm1
        old_residual old_add q0 v0 warm2 k0 old_norm warm22 scores0 warm15 old_turn warm4 exp0 shift0 k1
        q1 v1 scores1 turn0 shift1 warm18 scores2 pv0 shift2 warm4 exp1 exp2 scale0 turn1 warm1
        out_turn0 warm12 residual0 add0 warm2 scores3 pv1 shift3 exp3 warm10 scale1 turn2 warm3
        out_turn1 warm3 residual1 rstd0 add1 norm0 scale2 warm4 pv2 turn3 warm5 out_turn2 warm2
        residual2 add2 warm1 pv3 scale3 norm_turn0""",
    "ffn2": """old_sums old_probs_turn old_pv old_scale old_add warm3 old_last old_out_turn warm15
        old_residual old_rstd old_norm up0 old_turn warm4 up1 down0 down1 rstd0 norm0 down2 warm18
        norm_turn0""",
    "site6": """old_probs_turn old_sums old_pv old_scale ctx_turn0 warm1 q0 warm1 v0 k0 old_last
        old_out_turn old_residual old_rstd warm3 old_add warm3 scores0 warm1 old_norm old_turn shift0
        warm8 q1 exp0 ctx_turn1 warm8 k1 shift1 v1 scores1 turn0 exp1 warm11 scores2 shift2 pv0 exp2
        turn1 scale0 warm3 out_turn0 shift3 scale1 scores3 pv1 residual0 add0 exp3 turn2 warm1 out_turn1
        warm4 residual1 add1 norm0 rstd0 turn3 pv2 scale2 warm8 norm_turn0 out_turn2 warm7 residual2
        add2 pv3 scale3""",
    "site7": """old_probs_turn old_sums old_scale old_pv ctx_turn0 warm1 q0 warm1 v0 k0 old_out_turn
        old_residual old_rstd old_add warm6 scores0 warm2 old_last old_norm old_turn shift0 warm7 q1
        warm1 exp0 ctx_turn1 warm8 k1 shift1 v1 scores1 turn0 exp1 warm11 scores2 shift2 pv0 exp2 turn1
        scale0 out_turn0 shift3 warm3 scale1 add0 scores3 pv1 residual0 exp3 turn2 out_turn1 warm5
        residual1 add1 norm0 scale2 rstd0 pv2 turn3 warm4 norm_turn0 out_turn2 add2 warm7 residual2
        scale3 pv3""",
    "experts": """old_scale route0 pick0 old_probs_turn route1 pick1 old_last old_out_turn warm6
        old_residual warm8 old_add old_norm old_pv gate_exp0 old_rstd warm1 up0_0 warm3 old_turn gates0
        route2 warm2 pick2 route3 pick3 gate_exp1 down0_0 gates1 up0_1 gates_turn0 up1_0 gate_bias0
        gates_turn1 add_bias0 gate_bias1 add_bias1 down0_1 up1_1 add_bias2 gate_bias2 gate_bias3
        add_bias3""",
}
EXPERTS_AHEAD = 2
LATE = dict(old_last="last", old_probs_turn="turn3", old_sums="sums3", old_pv="pv3", old_scale="scale3",
            old_out_turn="out_turn3", old_residual="residual3", old_add="add3", old_rstd="rstd1",
            old_norm="norm1", old_turn="norm_turn1")


def schedule():
    old = {}

    def warm(name):
        return [("warm", int(name[4:]))]

    def attention(a):
        site, r = SITES[a], AFTER_SITE[a]
        step = dict(old)
        for u in range(NU):
            for kind in ("scores", "shift", "exp", "turn", "sums", "pv", "scale"):
                step[f"{kind}{u}"] = [(kind, a, u)]
            step[f"out_turn{u}"] = [("out_turn", a, u)] if site["out"] else []
            step[f"residual{u}"] = [("residual", a, r, u)] if site["out"] else []
            step[f"add{u}"] = [("add", a, r, u)]
        for s in range(NS):
            for kind in ("q", "k", "qk", "v", "lengths"):
                step[f"{kind}{s}"] = [(kind, a, s)]
            step[f"ctx_turn{s}"] = [("ctx_turn", a, s)] if a in CTX_TURNS else []
            step[f"rstd{s}"] = [("rstd", r, s)]
            masks = [("ctx_mask", 2 * s), ("ctx_mask", 2 * s + 1)] if a == 0 else []
            step[f"norm{s}"] = [("norm", r, s)] + masks
            step[f"norm_turn{s}"] = [("norm_turn", r, s)]
        step["last"] = []
        order = ORDER[f"site{a}"].split()
        for name, late in LATE.items():
            old[name] = step[late] if late not in order and (late != "sums3" or site["wide"]) else []
        return [x for name in order for x in (step[name] if name in step else warm(name))]

    def ffn(n):
        r = AFTER_FFN[n]
        last = LN_ONLY if n == 1 else r
        step = dict(old)
        for u in range(NU):
            step[f"down{u}"] = [("ffn_down", n, u)]
            step[f"stats{u}"] = [("stats", LN_ONLY, u)]
        for s in range(NS):
            step[f"up{s}"] = [("ffn_up", n, s)]
            step[f"rstd{s}"], step[f"norm{s}"] = [("rstd", r, s)], [("norm", r, s)]
            step[f"again_rstd{s}"], step[f"again_norm{s}"] = [("rstd", LN_ONLY, s)], [("norm", LN_ONLY, s)]
            step[f"norm_turn{s}"] = [("norm_turn", last, s)]
        norm = step["norm1"]
        if n == 1:
            norm = norm + step["stats2"] + step["stats3"] + step["again_rstd1"] + step["again_norm1"]
        old.update({name: [] for name in LATE})
        old.update(old_last=step["down3"], old_rstd=step["rstd1"], old_norm=norm, old_turn=step["norm_turn1"])
        return [x for name in ORDER[f"ffn{n}"].split() for x in (step[name] if name in step else warm(name))]

    steps = [("input_turn", 0), ("input_turn", 1), ("masks",)]
    old.update({name: [] for name in LATE})
    steps += attention(0) + attention(1) + ffn(0)
    steps += [("weights", 1)] + attention(2) + attention(3) + ffn(1)
    steps += [("weights", 2)] + attention(4) + attention(5) + [("ctx_rstd",), ("ctx_norm",)] + ffn(2)
    steps += [("weights", 3)] + attention(6) + attention(7)

    step = dict(old)
    for u in range(NU):
        for kind in ("route", "pick", "gate_bias", "add_bias"):
            step[f"{kind}{u}"] = [(kind, u)]
    for s in range(NS):
        for kind in ("gate_exp", "gates", "gates_turn"):
            step[f"{kind}{s}"] = [(kind, s)]
        for e in range(NE):
            step[f"up{e}_{s}"], step[f"down{e}_{s}"] = [("expert_up", e, s)], [("expert_down", e, s)]
    order = ORDER["experts"].split()
    steps += [("weights", 4), ("weights", 5)]
    for e in range(EXPERTS_AHEAD, NE):
        order += [f"down{e - 1}_0", f"up{e}_0", f"down{e - 1}_1", f"up{e}_1"]
    order += [f"down{NE - 1}_0", f"down{NE - 1}_1"]
    steps += [x for name in order for x in (step[name] if name in step else warm(name))]
    return steps



def weight_layout():
    at, n = {}, 0

    def put(name, width):
        nonlocal n
        at[name] = (n, width)
        n += width

    starts = []
    for layer in range(4):
        starts.append(n)
        for a in (2 * layer, 2 * layer + 1):
            w = H * DKB if SITES[a]["wide"] else D
            for k in ("q", "k", "v") + (("qp", "kp") if SITES[a]["rope"] else ()):
                put(f"w{k}{a}", w)
            if SITES[a]["out"]:
                put(f"wo{a}", w)
        if layer in FFN_WIDTH:
            put(f"up{layer}", FFN_WIDTH[layer])
            put(f"down{layer}", FFN_WIDTH[layer])
    put("router", NE)
    for e in range(NE):
        if e % 4 == 0:
            starts.append(n)
        put(f"up_e{e}", FF)
        put(f"down_e{e}", FF)
    return at, n, starts


def column_layout():
    at, n = {}, 0

    def put(name, width):
        nonlocal n
        at[name] = (n, width)
        n += width

    for r in range(len(NORMS)):
        put(f"g{r}", 1)
        put(f"b{r}", 1)
    put("gc", 1)
    put("bc", 1)
    for a in range(8):
        if SITES[a]["bias"]:
            w = HP if SITES[a]["wide"] else 1
            for k in ("q", "k") + (("qp", "kp") if SITES[a]["rope"] else ()):
                put(f"b{k}{a}", w)
    for n_, f in FFN_WIDTH.items():
        put(f"up_b{n_}", f // P)
    for e in range(NE):
        put(f"up_be{e}", FF // P)
    return at, n


def row_layout():
    at, n = {}, 0

    def put(name, width):
        nonlocal n
        at[name] = (n, width)
        n += width

    for r, norm in enumerate(NORMS):
        if norm["post"]:
            put(f"g{r}", D)
            put(f"b{r}", D)
        if norm["add"]:
            put(f"add{r}", D)
    for a in range(8):
        if SITES[a]["bias"]:
            put(f"bv{a}", H * DKB if SITES[a]["wide"] else D)
    put("down_b0", D)
    put("router_b", NE)
    return at, n


def constant_layout():
    at, n = {}, 0
    for name, width in (("ident", P), ("head_of_four", 4), ("causal", T), ("iota", T), ("head_of_all", 32),
                        ("own_head", H), ("own_rows", SB),
                        ("eps_small", 1), ("eps_large", 1),
                        ("cos", SW), ("sin", SW)):
        at[name] = (n, width)
        n += width
    return at, n


W_AT, W_N, W_PARTS = weight_layout()
C_AT, C_N = column_layout()
R_AT, R_N = row_layout()
K_AT, K_N = constant_layout()


class Ring:

    def __init__(self, banks, full, emptied):
        self.banks, self.full, self.emptied = banks, full, emptied
        self.at = {}

    def take(self, pe, name):
        n = len(self.at)
        k = n % len(self.banks)
        turn = n // len(self.banks) + 1
        self.at[name] = (k, turn)
        if turn > 1:
            pe.wait_ge(self.emptied[k], turn - 1)
        return self.banks[k]

    def spare(self, pe):
        n = len(self.at)
        k, turn = n % len(self.banks), n // len(self.banks) + 1
        if turn > 1:
            pe.wait_ge(self.emptied[k], turn - 1)
        return self.banks[k]

    def filled(self, name):
        return self.full[self.at[name][0]]

    def read(self, name):
        return self.emptied[self.at[name][0]]

    def wait_filled(self, engine, name):
        k, turn = self.at[name]
        engine.wait_ge(self.full[k], turn)
        return self.banks[k]

    def wait_read(self, engine, name):
        k, turn = self.at[name]
        engine.wait_ge(self.emptied[k], turn)


def decoder_stack(nc, x, ctx, mask, weights, columns, rows, constants, expert_bias, out):
    steps = schedule()
    with ExitStack() as stack:
        def sb(name, shape, dt=F32):
            return stack.enter_context(nc.sbuf_tensor(name, shape, dt))

        def sem(name):
            return stack.enter_context(nc.semaphore(name))

        w_sb = sb("w_sb", [P, W_N])
        col = sb("col", [P, C_N])
        row = sb("row", [P, R_N])
        const = sb("const", [P, K_N])
        expert_b = sb("expert_b", [NE, D])
        res = sb("res", [P, NU, D])
        raw = sb("raw", [P, NU, D])
        normed = sb("normed", [P, NU, D])
        c_tok = sb("c_tok", [P, NU, D])
        c_work = sb("c_work", [P, NU, D])
        scaled = sb("scaled", [P, 2, D])
        hT = sb("hT", [P, TOK])
        cT = sb("cT", [P, TOK])
        qT = sb("qT", [P, TOK])
        kT = sb("kT", [P, TOK])
        k4 = sb("k4", [P, 4, TOK])
        v8 = sb("v8", [P, NB * HP, 2 * (DK + 1)])
        qW = k4[:].rearrange("p j t -> p (j t)").rearrange("p (c t) -> p c t", c=HP)
        kW = sb("kW", [P, HP, SB, P])
        vW = sb("vW", [P, SB, HP, P])
        probs = sb("probs", [P, 2, H * T])
        pT = sb("pT", [P, 2, HP, P])
        att = sb("att", [P, 2, H * DKB])
        attT = sb("attT", [P, HP, P])
        hid = att[:].rearrange("p s (f t) -> p s f t", t=SW)
        rope_a = att[:, 0, 512:1024].rearrange("p (k t) -> p k t", k=2)
        rope_b = att[:, 1, 512:1024].rearrange("p (k t) -> p k t", k=2)
        len_mask = attT[:].rearrange("p c t -> p (c t)").bitcast(BF16).rearrange("p (s w) -> p s w", s=NS)
        mask_u8 = sb("mask_u8", [P, NU, T], U8)
        pad = sb("pad", [P, NU, T], BF16)
        pad_causal = sb("pad_causal", [P, NU, T], BF16)
        causal = sb("causal", [P, T], BF16)
        ident_half = sb("ident_half", [P, P], BF16)
        top = sb("top", [P, 2, H])
        largest = sb("largest", [P, 1])
        den = sb("den", [P, 2, H])
        first_q = sb("first_q", [P, SB, 32])
        own_rows = sb("own_rows", [P, SB, T], BF16)
        flags = sb("flags", [P, T])
        late = sb("late", [P, T])
        count = sb("count", [P, 1])
        valid = sb("valid", [P, 2, NU])
        tok_mask = sb("tok_mask", [P, 2, NU])
        stat6 = sb("stat6", [P, 6])
        stat = sb("stat", [P, 2 * NU, 2])
        log_var = sb("log_var", [P, 2 * NU])
        rstd = sb("rstd", [P, 2 * NU])
        newton = sb("newton", [P, 2 * NU])
        logits = sb("logits", [P, NU, NE])
        best = sb("best", [P, NU, NE])
        best_i = sb("best_i", [P, NU, NE], U32)
        best_f = sb("best_f", [P, NU, 2])
        share = sb("share", [P, NU, 4])
        one_hot = sb("one_hot", [P, 2, NU, NE])
        gates = sb("gates", [P, NU, NE])
        gatesT = pT[0:NE, 0, 0:NU, :]

        sc = stack.enter_context(nc.psum_tensor("sc", [P, 4, 512], F32))
        work = stack.enter_context(nc.psum_tensor("work", [P, 4, 512], F32))

        vectors_in = sem("vectors_in")
        part_in = [sem(f"weights_in{k}") for k in range(len(W_PARTS))]
        zeroed = sem("zeroed")
        ones_set = sem("ones_set")
        first_in = sem("first_in")
        next_in = sem("next_in")
        masks_read = sem("masks_read")
        masks_done = sem("masks_done")
        raw_free = sem("raw_free")
        k4_done = sem("k4_done")
        rope_done = sem("rope_done")
        scores_done = sem("scores_done")
        scores_read = sem("scores_read")
        first_q_done = sem("first_q_done")
        counted = sem("counted")
        len_masked = sem("len_masked")
        exp_done = sem("exp_done")
        stats_done = sem("stats_done")
        normed_done = sem("normed_done")
        res_done = sem("res_done")
        tok_masked = sem("tok_masked")
        ctx_masked = sem("ctx_masked")
        ctx_stats = sem("ctx_stats")
        ctx_normed = sem("ctx_normed")
        picked = sem("picked")
        gate_exp_done = sem("gate_exp_done")
        gates_done = sem("gates_done")
        vector_step = sem("vector_step")
        pool_step = sem("pool_step")
        scalar_step = sem("scalar_step")
        rstd_done = sem("rstd_done")
        ring = Ring([work[:, k, :] for k in range(4)], [sem(f"bank_filled{k}") for k in range(4)],
                    [sem(f"bank_read{k}") for k in range(4)])
        per_tile = [next_in, masks_read, masks_done, k4_done, rope_done, scores_done,
                    scores_read, first_q_done, counted, len_masked, exp_done, stats_done, normed_done, res_done,
                    tok_masked, ctx_masked, ctx_stats, ctx_normed, picked, gate_exp_done, gates_done,
                    vector_step, pool_step, scalar_step, rstd_done, *ring.full, *ring.emptied]

        def W(name, lo=0, n=None):
            at, width = W_AT[name]
            return w_sb[:, at + lo:at + (width if n is None else lo + n)]

        def COL(name, k=0):
            return col[:, C_AT[name][0] + k:C_AT[name][0] + k + 1]

        def ROW(name, lo=0, n=None):
            at, width = R_AT[name]
            return row[:, at + lo:at + (width if n is None else lo + n)]

        def K(name, lo=0, n=None):
            at, width = K_AT[name]
            return const[:, at + lo:at + (width if n is None else lo + n)]

        ident = K("ident")

        K4_N = {x: n + 1 for n, x in enumerate([s[1:] for s in steps if s[0] == "k"])}
        ROPE_N = {x: n + 1 for n, x in enumerate([s for s in steps if s[0] in ("q", "k") and SITES[s[1]]["rope"]])}
        NORM_N = {x: n + 1 for n, x in enumerate([s[1:] for s in steps if s[0] == "norm"])}
        RSTD_N = {x: n + 1 for n, x in enumerate([s for s in steps if s[0] in ("norm", "ctx_norm")])}
        LEN_N = {x: n + 1 for n, x in enumerate([s[1:] for s in steps if s[0] == "lengths"])}
        PICK_N = {x: n + 1 for n, x in enumerate([s[1] for s in steps if s[0] == "pick"])}
        GATES_N = {x: n + 1 for n, x in enumerate([s[1] for s in steps if s[0] == "gates"])}
        OUT_N = {x: n + 1 for n, x in enumerate([s[1:] for s in steps if s[0] == "out_turn"])}

        def wait_pv(engine, a, u):
            n = NU * a + u - 2
            if n >= 0:
                job = ("pv", n // NU, n % NU)
                ring.wait_filled(engine, job + (1,) if SITES[n // NU]["wide"] else job)

        def wait_att(engine, a, u):
            sites = [k for k in range(8) if SITES[k]["out"]]
            n = NU * sites.index(a) + u - 2
            pa, pu = sites[n // NU], n % NU
            ring.wait_filled(engine, ("out_turn", pa, pu, 1 if SITES[pa]["wide"] else 0))

        def token_major(tokens):
            return tokens.rearrange("u p d -> p u d")

        def load_masks(sp, t, done):
            of_unit = mask[t].rearrange("(u b) k -> b u k", b=2)
            for b in range(2):
                sp.dma_start(mask_u8[b * T:(b + 1) * T, :, :],
                             of_unit[b:b + 1].to_broadcast([T, NU, T])).then_inc(done, 16)

        with nc.Block() as block:
            @block.sync
            def _(sp):
                sp.dma_start(res[:], token_major(x[ITERS - 1])).then_inc(first_in, 16)
                sp.dma_start(c_tok[:], token_major(ctx[ITERS - 1])).then_inc(first_in, 16)
                load_masks(sp, ITERS - 1, first_in)
                sp.dma_start(const[:], constants[:, :]).then_inc(vectors_in, 16)
                sp.dma_start(col[:], columns[:, :]).then_inc(vectors_in, 16)
                sp.dma_start(row[:], rows[:, :].to_broadcast([P, R_N])).then_inc(vectors_in, 16)
                sp.dma_start(expert_b[:], expert_bias[:, :]).then_inc(vectors_in, 16)
                for k, lo in enumerate(W_PARTS):
                    hi = W_PARTS[k + 1] if k + 1 < len(W_PARTS) else W_N
                    sp.dma_start(w_sb[:, lo:hi], weights[:, lo:hi]).then_inc(part_in[k], 16)
                sp.wait_ge(first_in, 16 * 4)
                sp.wait_ge(vectors_in, 16 * 4)
                sp.wait_ge(part_in[0], 16)

            @block.gpsimd
            def _(pool):
                pool.memset(kW[:], 0.0).then_inc(zeroed, 1)

            @block.vector
            def _(dve):
                dve.memset(raw[:], 0.0).then_inc(raw_free, 16)
                dve.memset(vW[:], 0.0).then_inc(zeroed, 1)
                dve.memset(v8[:], 0.0).then_inc(zeroed, 1)
                dve.wait_ge(zeroed, 3)
                dve.memset(v8[0:T, :, DK:DK + 1], 1.0).then_inc(ones_set, 1)
                dve.memset(v8[T:P, :, 2 * DK + 1:2 * DK + 2], 1.0).then_inc(ones_set, 1)
                dve.wait_ge(vectors_in, 16 * 4)
                dve.tensor_copy(own_rows[:], K("own_rows").rearrange("p (b o) -> p b o", o=1)
                                .to_broadcast([P, SB, T])).then_inc(ones_set, 1)
                dve.tensor_copy(causal[:], K("causal")).then_inc(ones_set, 1)
                dve.tensor_copy(ident_half[:], ident).then_inc(ones_set, 1)

        with nc.Fori(0, ITERS) as tile:
            with nc.Block() as block:

                @block.tensor
                def _(pe):
                    def kv_of(a):
                        return cT if SITES[a]["cross"] else hT

                    def for_heads(m, n):
                        return m.rearrange("p (o k) -> p o k", o=1).to_broadcast([P, n, T])

                    def wait_source(step):
                        for turn in SOURCE[step]:
                            ring.wait_read(pe, turn)

                    SOURCE = {}
                    last_h = {s: ("input_turn", s) for s in range(NS)}
                    last_c = {}
                    for step in steps:
                        if step[0] == "norm_turn":
                            last_h[step[2]] = step
                        if step[0] == "ctx_turn":
                            last_c[step[2]] = step
                        if step[0] in ("qk", "q", "k", "v"):
                            cross = SITES[step[1]]["cross"]
                            SOURCE[step] = [last_h[step[2]]] if step[0] in ("qk", "q") or not cross else []
                            SOURCE[step] += [last_c[step[2]]] if step[0] != "q" and cross else []

                    def turn_stream(step, src, s):
                        bank = ring.take(pe, step)
                        for j in range(2):
                            i = nc.tensor.transpose(bank[:, j * P:(j + 1) * P], src[:, 2 * s + j, :], ident)
                        i.then_inc(ring.filled(step), 1)

                    h_now = {}
                    for step in steps:
                        kind = step[0]
                        if kind == "weights":
                            pe.wait_ge(part_in[step[1]], 16)
                        elif kind == "warm":
                            bank = ring.spare(pe)
                            some = own_rows[:].rearrange("p b t -> p (b t)")
                            for _ in range(step[1]):
                                nc.tensor.matmul(bank[:, 0:SB * T], some[:, 0:P], some, start=True, stop=True)
                        elif kind == "input_turn":
                            s = step[1]
                            turn_stream(step, res, s)
                            h_now[s] = step
                        elif kind == "norm_turn":
                            r, s = step[1:]
                            pe.wait_ge(normed_done, NORM_N[(r, s)])
                            turn_stream(step, normed, s)
                            h_now[s] = step
                        elif kind == "ctx_turn":
                            a, s = step[1:]
                            if a == 1:
                                pe.wait_ge(ctx_masked, 2 * s + 2)
                                turn_stream(step, c_work, s)
                            elif a == 7:
                                pe.wait_ge(ctx_normed, 1)
                                turn_stream(step, c_work, s)
                            else:
                                turn_stream(step, c_tok, s)
                        elif kind == "qk":
                            a, s = step[1:]
                            wait_source(step)
                            cols = slice(s * SW, (s + 1) * SW)
                            for c in range(HP):
                                for name, src in (("q", hT), ("k", kv_of(a))):
                                    job = step + (name, c)
                                    bank = ring.take(pe, job)
                                    nc.tensor.matmul(bank[:, 0:SW], W(f"w{name}{a}", c * P, P), src[:, cols],
                                                     start=True, stop=True).then_inc(ring.filled(job), 1)
                        elif kind in ("q", "k"):
                            a, s = step[1:]
                            wait_source(step)
                            src = hT if kind == "q" else kv_of(a)
                            for name in (kind, kind + "p") if SITES[a]["rope"] else (kind,):
                                job = step + (name,)
                                bank = ring.take(pe, job)
                                nc.tensor.matmul(bank[:, 0:SW], W(f"w{name}{a}"), src[:, s * SW:(s + 1) * SW],
                                                 start=True, stop=True).then_inc(ring.filled(job), 1)
                        elif kind == "v":
                            a, s = step[1:]
                            wait_source(step)
                            w = H * DKB // 2 if SITES[a]["wide"] else D // 2
                            if SITES[a]["wide"]:
                                for b in range(SB):
                                    job = step + (b,)
                                    bank = ring.take(pe, job)
                                    tok = kv_of(a)[:, s * SW + b * T:s * SW + (b + 1) * T]
                                    for half in range(2):
                                        i = nc.tensor.matmul(bank[half * T:(half + 1) * T, 0:w], tok,
                                                             W(f"wv{a}", half * w, w), start=True, stop=True)
                                    i.then_inc(ring.filled(job), 1)
                            else:
                                bank = ring.take(pe, step)
                                for b in range(SB):
                                    tok = kv_of(a)[:, s * SW + b * T:s * SW + (b + 1) * T]
                                    for half in range(2):
                                        i = nc.tensor.matmul(bank[half * T:(half + 1) * T, b * w:(b + 1) * w], tok,
                                                             W(f"wv{a}", half * w, w), start=True, stop=True)
                                i.then_inc(ring.filled(step), 1)
                        elif kind == "scores":
                            a, u = step[1:]
                            n = NU * a + u
                            s = u // 2
                            free = n - 1 if SITES[a]["wide"] and u > 0 else n
                            if free > 0:
                                pe.wait_ge(scores_read, free)
                            if SITES[a]["wide"]:
                                pe.wait_ge(masks_done, 1)
                                m = (pad_causal if SITES[a]["causal"] else pad)[:, u, :]
                                for g in range(2):
                                    nc.tensor.matmul(sc[:, 2 * (u % 2) + g, :], ident_half[:], for_heads(m, HP),
                                                     start=True, stop=False, skip_group_check=True)
                                for c in range(HP):
                                    if u % 2 == 0:
                                        ring.wait_read(pe, ("qk", a, s, "q", c))
                                        ring.wait_read(pe, ("qk", a, s, "k", c))
                                    for b in range(2):
                                        bb = 2 * (u % 2) + b
                                        at = (c % 4) * P
                                        i = nc.tensor.matmul(sc[b * T:(b + 1) * T, 2 * (u % 2) + c // 4, at:at + P],
                                                             qW[:, c, bb * T:(bb + 1) * T], kW[:, c, bb, :],
                                                             start=False, stop=True, skip_group_check=True)
                            else:
                                if u % 2 == 0:
                                    pe.wait_ge(k4_done, K4_N[(a, s)])
                                    if SITES[a]["rope"]:
                                        pe.wait_ge(rope_done, ROPE_N[("q", a, s)])
                                    else:
                                        ring.wait_read(pe, ("q", a, s, "q"))
                                masked = SITES[a]["lengths"] or SITES[a]["causal"]
                                if SITES[a]["lengths"]:
                                    pe.wait_ge(len_masked, LEN_N[(a, s)])
                                    pair = own_rows[:, 2 * (u % 2):2 * (u % 2) + 2, :].rearrange("p b t -> p (b t)")
                                    for g in range(4):
                                        nc.tensor.matmul(sc[:, g, 0:256], pair, len_mask[:, s, g * 256:(g + 1) * 256],
                                                         start=True, stop=False, skip_group_check=True)
                                if SITES[a]["causal"]:
                                    for g in range(4):
                                        nc.tensor.matmul(sc[:, g, 0:256], ident_half[:], for_heads(causal[:], 4),
                                                         start=not SITES[a]["lengths"], stop=False,
                                                         skip_group_check=True)
                                for b in range(2):
                                    tok = slice((2 * u + b) * T, (2 * u + b + 1) * T)
                                    for g in range(4):
                                        rows_ = slice(32 * g, 32 * g + 32)
                                        i = nc.tensor.matmul(sc[b * T:(b + 1) * T, g, 0:256],
                                                             qT[rows_, tok], k4[rows_, :, tok],
                                                             start=not masked, stop=True,
                                                             skip_group_check=masked)
                            i.then_inc(scores_done, 1)
                        elif kind == "lengths":
                            a, s = step[1:]
                            ring.wait_read(pe, ("k", a, s, "k"))
                            pe.wait_ge(first_q_done, LEN_N[(a, s)])
                            bank = ring.take(pe, step)
                            for b in range(SB):
                                i = nc.tensor.matmul(bank[32 * b:32 * b + 32, 0:T], first_q[:, b, :],
                                                     kT[:, s * SW + b * T:s * SW + (b + 1) * T], start=True,
                                                     stop=True)
                            i.then_inc(ring.filled(step), 1)
                        elif kind == "turn":
                            a, u = step[1:]
                            pe.wait_ge(exp_done, NU * a + u + 1)
                            for half in range(2):
                                job = step + (half,)
                                bank = ring.take(pe, job)
                                for c in range(4):
                                    hp = 4 * half + c
                                    i = nc.tensor.transpose(bank[:, c * P:(c + 1) * P],
                                                            probs[:, u % 2, hp * P:(hp + 1) * P], ident)
                                i.then_inc(ring.filled(job), 1)
                        elif kind == "pv":
                            a, u = step[1:]
                            s = u // 2
                            for b in range(SB if SITES[a]["wide"] else 1):
                                ring.wait_read(pe, ("v", a, s, b) if SITES[a]["wide"] else ("v", a, s))
                            if SITES[a]["wide"]:
                                for half in range(2):
                                    ring.wait_read(pe, ("turn", a, u, half))
                                    job = step + (half,)
                                    bank = ring.take(pe, job)
                                    for c in range(4):
                                        hp = 4 * half + c
                                        for b in range(2):
                                            i = nc.tensor.matmul(bank[b * T:(b + 1) * T, c * P:(c + 1) * P],
                                                                 pT[:, u % 2, hp, b * T:(b + 1) * T],
                                                                 vW[:, 2 * (u % 2) + b, hp, :],
                                                                 start=True, stop=True)
                                    i.then_inc(ring.filled(job), 1)
                            else:
                                w = 2 * (DK + 1)
                                bank = ring.take(pe, step)
                                for half in range(2):
                                    ring.wait_read(pe, ("turn", a, u, half))
                                    for c in range(4):
                                        hp = 4 * half + c
                                        for b in range(2):
                                            i = nc.tensor.matmul(bank[b * T:(b + 1) * T, hp * w:(hp + 1) * w],
                                                                 pT[:, u % 2, hp, b * T:(b + 1) * T],
                                                                 v8[:, (2 * u + b) * HP + hp, :],
                                                                 start=True, stop=True)
                                i.then_inc(ring.filled(step), 1)
                        elif kind == "out_turn":
                            a, u = step[1:]
                            for half in range(2 if SITES[a]["wide"] else 1):
                                ring.wait_read(pe, ("pv", a, u, half) if SITES[a]["wide"] else ("pv", a, u))
                            if SITES[a]["wide"]:
                                for half in range(2):
                                    job = step + (half,)
                                    bank = ring.take(pe, job)
                                    for c in range(4):
                                        hp = 4 * half + c
                                        i = nc.tensor.transpose(bank[:, c * P:(c + 1) * P],
                                                                att[:, u % 2, hp * P:(hp + 1) * P], ident)
                                    i.then_inc(ring.filled(job), 1)
                            else:
                                bank = ring.take(pe, step + (0,))
                                nc.tensor.transpose(bank[:, 0:P], att[:, u % 2, 0:P],
                                                    ident).then_inc(ring.filled(step + (0,)), 1)
                        elif kind == "residual":
                            a, r, u = step[1:]
                            bank = ring.take(pe, step)
                            chunks = HP if SITES[a]["wide"] else 1
                            for c in range(chunks):
                                if c % 4 == 0:
                                    ring.wait_read(pe, ("out_turn", a, u, c // 4))
                                i = nc.tensor.matmul(bank[:, 0:D], attT[:, c, :],
                                                     W(f"wo{a}", c * D, D), start=c == 0, stop=c == chunks - 1)
                            i.then_inc(ring.filled(step), 1)
                        elif kind == "ffn_up":
                            n, s = step[1:]
                            ring.wait_read(pe, h_now[s])
                            for f in range(FFN_WIDTH[n] // P):
                                job = step + (f,)
                                bank = ring.take(pe, job)
                                nc.tensor.matmul(bank[:, 0:SW], W(f"up{n}", f * P, P), hT[:, s * SW:(s + 1) * SW],
                                                 start=True, stop=True).then_inc(ring.filled(job), 1)
                        elif kind == "ffn_down":
                            n, u = step[1:]
                            nf = FFN_WIDTH[n] // P
                            bank = ring.take(pe, step)
                            for f in range(nf):
                                ring.wait_read(pe, ("ffn_up", n, u // 2, f))
                                i = nc.tensor.matmul(bank[:, 0:D], hid[:, u // 2, f, (u % 2) * P:(u % 2 + 1) * P],
                                                     W(f"down{n}", f * D, D), start=f == 0, stop=f == nf - 1)
                            i.then_inc(ring.filled(step), 1)
                        elif kind == "route":
                            u = step[1]
                            ring.wait_read(pe, h_now[u // 2])
                            bank = ring.take(pe, step)
                            nc.tensor.matmul(bank[:, 0:NE], hT[:, u * P:(u + 1) * P], W("router"), start=True,
                                             stop=True).then_inc(ring.filled(step), 1)
                        elif kind == "gates_turn":
                            s = step[1]
                            pe.wait_ge(gates_done, GATES_N[s])
                            bank = ring.take(pe, step)
                            for j in range(2):
                                i = nc.tensor.transpose(bank[0:NE, j * P:(j + 1) * P], gates[:, 2 * s + j, :], ident)
                            i.then_inc(ring.filled(step), 1)
                        elif kind == "gate_bias":
                            u = step[1]
                            ring.wait_read(pe, ("gates_turn", u // 2))
                            bank = ring.take(pe, step)
                            nc.tensor.matmul(bank[:, 0:D], gatesT[:, u, :], expert_b[:], start=True,
                                             stop=True).then_inc(ring.filled(step), 1)
                        elif kind == "expert_up":
                            e, s = step[1:]
                            ring.wait_read(pe, h_now[s])
                            for f in range(FF // P):
                                job = step + (f,)
                                bank = ring.take(pe, job)
                                nc.tensor.matmul(bank[:, 0:SW], W(f"up_e{e}", f * P, P),
                                                 hT[:, s * SW:(s + 1) * SW], start=True,
                                                 stop=True).then_inc(ring.filled(job), 1)
                        elif kind == "expert_down":
                            e, s = step[1:]
                            for j in range(2):
                                job = step + (j,)
                                bank = ring.take(pe, job)
                                for f in range(FF // P):
                                    if j == 0:
                                        ring.wait_read(pe, ("expert_up", e, s, f))
                                    i = nc.tensor.matmul(bank[:, 0:D], hid[:, s, f, j * P:(j + 1) * P],
                                                         W(f"down_e{e}", f * D, D), start=f == 0,
                                                         stop=f == FF // P - 1)
                                i.then_inc(ring.filled(job), 1)

                @block.scalar
                def _(act):
                    steps_done = [0]

                    def link(i):
                        steps_done[0] += 1
                        i.then_inc(scalar_step, 1)
                        act.wait_ge(scalar_step, steps_done[0])

                    act.preload_act_table_set("natural_log_exp_and_others")
                    for step in steps:
                        kind = step[0]
                        if kind in ("rstd", "ctx_rstd"):
                            if kind == "rstd":
                                act.wait_ge(stats_done, NORM_N[step[1:]])
                                units, eps = slice(2 * step[2], 2 * step[2] + 2), NORMS[step[1]]["eps"]
                            else:
                                act.wait_ge(ctx_stats, 1)
                                units, eps = slice(NU, 2 * NU), CTX_NORM["eps"]
                            link(nc.scalar.activation(log_var[:, units], stat[:, units, 1], ACT.Ln,
                                                      bias=K("eps_small" if eps == EPS_SMALL else "eps_large")))
                            nc.scalar.activation(rstd[:, units], log_var[:, units], ACT.Exp, scale=-0.5)\
                                .then_inc(rstd_done, 1)
                        elif kind in ("input_turn", "norm_turn", "ctx_turn"):
                            s = step[-1]
                            bank = ring.wait_filled(act, step)
                            cols = slice(s * SW, (s + 1) * SW)
                            if kind == "input_turn" or (kind == "ctx_turn" and step[1] != 7):
                                dst = hT if kind == "input_turn" else cT
                                i = nc.scalar.activation(dst[:, cols], bank[:, 0:SW], ACT.Copy)
                            else:
                                dst, g, b = (cT, "gc", "bc") if kind == "ctx_turn" else (hT, f"g{step[1]}", f"b{step[1]}")
                                i = nc.scalar.activation(dst[:, cols], bank[:, 0:SW], ACT.Identity,
                                                         scale=COL(g), bias=COL(b))
                            i.then_inc(ring.read(step), 1)
                        elif kind == "qk":
                            a, s = step[1:]
                            for c in range(HP):
                                job = step + ("q", c)
                                bank = ring.wait_filled(act, job)
                                nc.scalar.activation(qW[:, c, :], bank[:, 0:SW], ACT.Identity,
                                                     bias=COL(f"bq{a}", c)).then_inc(ring.read(job), 1)
                        elif kind in ("q", "k") and not SITES[step[1]]["rope"]:
                            a, s = step[1:]
                            dst = (qT if kind == "q" else kT)[:, s * SW:(s + 1) * SW]
                            job = step + (kind,)
                            bank = ring.wait_filled(act, job)
                            if SITES[a]["bias"]:
                                i = nc.scalar.activation(dst, bank[:, 0:SW], ACT.Identity, bias=COL(f"b{kind}{a}"))
                            else:
                                i = nc.scalar.activation(dst, bank[:, 0:SW], ACT.Copy)
                            i.then_inc(ring.read(job), 1)
                        elif kind == "exp":
                            a, u = step[1:]
                            n = NU * a + u
                            act.wait_ge(scores_read, n + 1)
                            dk = DKB if SITES[a]["wide"] else DK
                            nc.scalar.activation(probs[:, u % 2, :], probs[:, u % 2, :], ACT.Exp,
                                                 scale=float(dk) ** -0.5).then_inc(exp_done, 1)
                        elif kind == "turn":
                            a, u = step[1:]
                            wait_pv(act, a, u)
                            for half in range(2):
                                bank = ring.wait_filled(act, step + (half,))
                                nc.scalar.activation(pT[:, u % 2, 4 * half:4 * half + 4, :], bank, ACT.Copy)\
                                    .then_inc(ring.read(step + (half,)), 1)
                        elif kind == "out_turn":
                            a, u = step[1:]
                            if u >= 1:
                                ring.wait_filled(act, ("residual", a, AFTER_SITE[a], u - 1))
                            for half in range(2 if SITES[a]["wide"] else 1):
                                job = step + (half,)
                                bank = ring.wait_filled(act, job)
                                w = 4 if SITES[a]["wide"] else 1
                                nc.scalar.activation(attT[:, 4 * half:4 * half + w, :],
                                                     bank[:, 0:w * P], ACT.Copy).then_inc(ring.read(job), 1)
                        elif kind in ("ffn_up", "expert_up"):
                            n, s = step[1:]
                            width = FFN_WIDTH[n] if kind == "ffn_up" else FF
                            if kind == "expert_up":
                                fn, bias = ACT.Gelu, f"up_be{n}"
                                if n > 0:
                                    ring.wait_filled(act, ("expert_down", n - 1, s, 1))
                            else:
                                fn, bias = (ACT.Gelu_apprx_tanh if n == 2 else ACT.Relu), f"up_b{n}"
                            for f in range(width // P):
                                job = step + (f,)
                                bank = ring.wait_filled(act, job)
                                nc.scalar.activation(hid[:, s, f, :], bank[:, 0:SW], fn,
                                                     bias=COL(bias, f)).then_inc(ring.read(job), 1)
                            if step == ("ffn_up", 2, NS - 1):
                                act.preload_act_table_set("natural_log_exp_and_others")
                        elif kind == "gate_exp":
                            s = step[1]
                            act.wait_ge(picked, PICK_N[2 * s + 1])
                            nc.scalar.activation(share[:, 2 * s:2 * s + 2, 1], share[:, 2 * s:2 * s + 2, 0], ACT.Exp)\
                                .then_inc(gate_exp_done, 1)
                        elif kind == "gates_turn":
                            s = step[1]
                            bank = ring.wait_filled(act, step)
                            nc.scalar.activation(gatesT[:, 2 * s:2 * s + 2, :], bank[0:NE, 0:SW], ACT.Copy)\
                                .then_inc(ring.read(step), 1)

                @block.vector
                def _(dve):
                    steps_done = [0]

                    def link(i):
                        steps_done[0] += 1
                        i.then_inc(vector_step, 1)
                        dve.wait_ge(vector_step, steps_done[0])

                    def statistics(src, u, done=None, at=0):
                        link(nc.vector.bn_stats(stat6[:], src[:, u, :]))
                        i = nc.vector.bn_aggr(stat[:, at + u, :], stat6[:])
                        if done is None:
                            link(i)
                        else:
                            i.then_inc(done, 1)

                    def refine(units, eps, n):
                        dve.wait_ge(rstd_done, n)
                        r1, t1 = rstd[:, units], newton[:, units]
                        link(nc.vector.scalar_tensor_tensor(t1, stat[:, units, 1], eps, r1, ALU.add, ALU.mult))
                        link(nc.vector.scalar_tensor_tensor(t1, t1, -0.5, r1, ALU.mult, ALU.mult))
                        link(nc.vector.scalar_tensor_tensor(t1, t1, 1.5, r1, ALU.add, ALU.mult))

                    def heads(ap, k=T):
                        return ap.rearrange("p (h k) -> p h k", k=k)

                    def over_keys(ap):
                        return ap.rearrange("p (h o) -> p h o", o=1).to_broadcast([P, H, T])

                    for step in steps:
                        kind = step[0]
                        if kind == "masks":
                            for u in range(NU):
                                link(nc.vector.tensor_reduce(largest[:], res[:, u, :], X_AXIS, ALU.max,
                                                             apply_absolute_value=True))
                                link(nc.vector.tensor_scalar(tok_mask[:, 0, u:u + 1], largest[:], 0.0, None,
                                                             ALU.is_gt))
                            nc.vector.tensor_scalar(pad[:], mask_u8[:], -1.0, BIG, ALU.add, ALU.mult)\
                                .then_inc(masks_read, 1)
                            dve.wait_ge(masks_read, 1)
                            some_causal = K("causal").rearrange("p (o k) -> p o k", o=1).to_broadcast([P, NU, T])
                            link(nc.vector.tensor_tensor(pad_causal[:], pad[:], some_causal, ALU.add))
                            for k, m in enumerate((pad, pad_causal)):
                                link(nc.vector.tensor_reduce(valid[:, k, :], m[:], X_AXIS, ALU.max))
                            nc.vector.tensor_scalar(valid[:], valid[:], -BIG / 2, None, ALU.is_gt)\
                                .then_inc(masks_done, 1)
                            dve.wait_ge(masks_done, 1)
                        elif kind == "qk":
                            a, s = step[1:]
                            for c in range(HP):
                                job = step + ("k", c)
                                bank = ring.wait_filled(dve, job)
                                for half in range(2):
                                    ps = slice(half * T, (half + 1) * T)
                                    i = nc.vector.tensor_scalar(
                                        kW[ps, c, :, ps], bank[ps, 0:SW].rearrange("p (b t) -> p b t", t=T),
                                        COL(f"bk{a}", c)[ps], None, ALU.add)
                                i.then_inc(ring.read(job), 1)
                        elif kind in ("q", "k"):
                            a, s = step[1:]
                            cols = slice(s * SW, (s + 1) * SW)
                            if SITES[a]["rope"]:
                                n, k = ROPE_N[step], int(kind == "k")
                                before = [m for x, m in ROPE_N.items() if x[0] == kind and m < n]
                                if before:
                                    dve.wait_ge(rope_done, max(before))
                                for part, table, buf in ((kind, "cos", rope_a), (kind + "p", "sin", rope_b)):
                                    job = step + (part,)
                                    bank = ring.wait_filled(dve, job)
                                    nc.vector.scalar_tensor_tensor(
                                        buf[:, k, :], bank[:, 0:SW], COL(f"b{part}{a}"), K(table),
                                        ALU.add, ALU.mult).then_inc(ring.read(job), 1)
                            if kind == "k":
                                if SITES[a]["rope"]:
                                    dve.wait_ge(rope_done, ROPE_N[step])
                                else:
                                    ring.wait_read(dve, step + ("k",))
                                for j in range(4):
                                    i = nc.vector.tensor_scalar(k4[:, j, cols], kT[:, cols], K("head_of_four", j, 1),
                                                                None, ALU.mult)
                                i.then_inc(k4_done, 1)
                        elif kind == "lengths":
                            a, s = step[1:]
                            ring.wait_read(dve, ("q", a, s, "q"))
                            q0 = qT[:, s * SW:(s + 1) * SW:T].rearrange("p (b o) -> p b o", o=1)
                            nc.vector.tensor_tensor(
                                first_q[:], K("head_of_all").rearrange("p (o h) -> p o h", o=1).to_broadcast([P, SB, 32]),
                                q0.to_broadcast([P, SB, 32]), ALU.mult).then_inc(first_q_done, 1)
                            bank = ring.wait_filled(dve, step)
                            nc.vector.tensor_scalar(flags[:], bank[:, 0:T], 0.0, None, ALU.not_equal)\
                                .then_inc(ring.read(step), 1)
                            ring.wait_read(dve, step)
                            link(nc.vector.tensor_reduce(count[:], flags[:], X_AXIS, ALU.add))
                            if LEN_N[(a, s)] > 1:
                                dve.wait_ge(len_masked, LEN_N[(a, s)] - 1)
                            nc.vector.tensor_scalar(late[:], K("iota"), count[:], -BIG, ALU.is_ge, ALU.mult)\
                                .then_inc(counted, 1)
                        elif kind == "v":
                            a, s = step[1:]
                            if SITES[a]["wide"]:
                                w = H * DKB // 2
                                for b in range(SB):
                                    job = step + (b,)
                                    bank = ring.wait_filled(dve, job)
                                    for half in range(2):
                                        ps = slice(half * T, (half + 1) * T)
                                        i = nc.vector.tensor_tensor(
                                            vW[ps, b, :, ps], bank[ps, 0:w].rearrange("p (h d) -> p h d", d=DKB),
                                            ROW(f"bv{a}", half * w, w)[ps].rearrange("p (h d) -> p h d", d=DKB),
                                            ALU.add)
                                    i.then_inc(ring.read(job), 1)
                            else:
                                bank = ring.wait_filled(dve, step)
                                w = D // 2
                                for half in range(2):
                                    ps = slice(half * T, (half + 1) * T)
                                    lo = half * (DK + 1)
                                    dst = v8[ps, s * SB * HP:(s + 1) * SB * HP, lo:lo + DK]
                                    src = bank[ps, 0:SB * w].rearrange("p (h d) -> p h d", d=DK)
                                    if SITES[a]["bias"]:
                                        dst = dst.rearrange("p (b h) d -> p b h d", b=SB)
                                        src = src.rearrange("p (b h) d -> p b h d", b=SB)
                                        bias = ROW(f"bv{a}", half * w, w)[ps].rearrange("p (o h d) -> p o h d", o=1, d=DK)
                                        i = nc.vector.tensor_tensor(dst, src, bias.to_broadcast([T, SB, HP, DK]),
                                                                    ALU.add)
                                    else:
                                        i = nc.vector.tensor_copy(dst, src)
                                i.then_inc(ring.read(step), 1)
                        elif kind == "shift":
                            a, u = step[1:]
                            n = NU * a + u
                            if SITES[a]["wide"]:
                                S = sc[:, 2 * (u % 2):2 * (u % 2) + 2, :]
                            else:
                                S = sc[:, :, 0:256]
                            banks = S.shape[1]
                            S4 = S.rearrange("p g (j k) -> p g j k", k=T)
                            dve.wait_ge(scores_done, n + 1)
                            if n >= 2:
                                m = n - 2
                                ring.wait_filled(dve, ("turn", m // NU, m % NU, 1))
                            link(nc.vector.tensor_reduce(top[:, u % 2, :].rearrange("p (g j) -> p g j", g=banks), S4, X_AXIS,
                                                         ALU.max))
                            top4 = top[:, u % 2, :].rearrange("p (g j o) -> p g j o", g=banks, o=1)
                            nc.vector.tensor_tensor(
                                probs[:, u % 2, :].rearrange("p (g j k) -> p g j k", g=banks, k=T), S4,
                                top4.to_broadcast([P, banks, H // banks, T]), ALU.subtract).then_inc(scores_read, 1)
                        elif kind == "sums":
                            a, u = step[1:]
                            dve.wait_ge(exp_done, NU * a + u + 1)
                            link(nc.vector.tensor_reduce(den[:, u % 2, :], heads(probs[:, u % 2, :]), X_AXIS, ALU.add))
                        elif kind == "scale":
                            a, u = step[1:]
                            den_u = den[:, u % 2, :]
                            if SITES[a]["wide"]:
                                some_key = valid[:, int(SITES[a]["causal"]), u:u + 1]
                                link(nc.vector.reciprocal(den_u, den_u))
                                link(nc.vector.tensor_scalar(den_u, den_u, some_key, None, ALU.mult))
                                if OUT_N[(a, u)] > 2:
                                    wait_att(dve, a, u)
                                for half in range(2):
                                    job = ("pv", a, u, half)
                                    bank = ring.wait_filled(dve, job)
                                    r8 = den_u[:, 8 * half:8 * half + 8].rearrange("p (h o) -> p h o", o=1)
                                    nc.vector.tensor_tensor(
                                        att[:, u % 2, 512 * half:512 * half + 512].rearrange("p (h d) -> p h d", d=DKB),
                                        bank.rearrange("p (h d) -> p h d", d=DKB), r8.to_broadcast([P, 8, DKB]),
                                        ALU.mult).then_inc(ring.read(job), 1)
                                ring.wait_read(dve, job)
                            else:
                                bank = ring.wait_filled(dve, ("pv", a, u))
                                o9 = bank[:, 0:H * (DK + 1)].rearrange("p (h d) -> p h d", d=DK + 1)
                                link(nc.vector.reciprocal(den_u.rearrange("p (h o) -> p h o", o=1), o9[:, :, DK:DK + 1]))
                                if SITES[a]["lengths"]:
                                    if a == 1:
                                        dve.wait_ge(tok_masked, u + 1)
                                    link(nc.vector.tensor_scalar(den_u, den_u, tok_mask[:, a, u:u + 1], None,
                                                                 ALU.mult))
                                dst = scaled[:, u % 2, :] if SITES[a]["lengths"] else att[:, u % 2, 0:P]
                                if not SITES[a]["lengths"] and OUT_N[(a, u)] > 2:
                                    wait_att(dve, a, u)
                                r8 = den_u.rearrange("p (h o) -> p h o", o=1).to_broadcast([P, H, DK])
                                nc.vector.tensor_tensor(dst.rearrange("p (h d) -> p h d", d=DK), o9[:, :, 0:DK], r8,
                                                        ALU.mult).then_inc(ring.read(("pv", a, u)), 1)
                                ring.wait_read(dve, ("pv", a, u))
                        elif kind == "add":
                            a, r, u = step[1:]
                            job = ("residual", a, r, u)
                            if r == 0 and u == 0:
                                dve.wait_ge(raw_free, 16 * tile + 16)
                            if r > 0:
                                dve.wait_ge(res_done, NORM_N[(r - 1, u // 2)])
                            if SITES[a]["out"]:
                                bank = ring.wait_filled(dve, job)
                                nc.vector.tensor_tensor(raw[:, u, :], bank[:, 0:D], res[:, u, :], ALU.add)\
                                    .then_inc(ring.read(job), 1)
                                ring.wait_read(dve, job)
                            else:
                                link(nc.vector.tensor_tensor(raw[:, u, :], scaled[:, u % 2, :], res[:, u, :], ALU.add))
                            statistics(raw, u, stats_done if u % 2 else None)
                        elif kind == "ffn_down":
                            n, u = step[1:]
                            r = AFTER_FFN[n]
                            dve.wait_ge(res_done, NORM_N[(r - 1, u // 2)])
                            bank = ring.wait_filled(dve, step)
                            if n == 0:
                                nc.vector.tensor_tensor(scaled[:, u % 2, :], bank[:, 0:D], ROW("down_b0"), ALU.add)\
                                    .then_inc(ring.read(step), 1)
                                ring.wait_read(dve, step)
                                link(nc.vector.scalar_tensor_tensor(raw[:, u, :], scaled[:, u % 2, :],
                                                                    tok_mask[:, 0, u:u + 1], res[:, u, :], ALU.mult,
                                                                    ALU.add))
                            else:
                                nc.vector.tensor_tensor(raw[:, u, :], bank[:, 0:D], res[:, u, :], ALU.add)\
                                    .then_inc(ring.read(step), 1)
                                ring.wait_read(dve, step)
                            statistics(raw, u, stats_done if u % 2 else None)
                        elif kind == "stats":
                            r, u = step[1:]
                            dve.wait_ge(res_done, NORM_N[(r - 1, u // 2)])
                            statistics(res, u, stats_done if u % 2 else None)
                        elif kind == "norm":
                            r, s = step[1:]
                            src = res if r == LN_ONLY else raw
                            refine(slice(2 * s, 2 * s + 2), NORMS[r]["eps"], RSTD_N[step])
                            for u in (2 * s, 2 * s + 1):
                                i = nc.vector.tensor_scalar(normed[:, u, :], src[:, u, :], stat[:, u, 0:1],
                                                            newton[:, u:u + 1], ALU.subtract, ALU.mult)
                            i.then_inc(normed_done, 1)
                            dve.wait_ge(normed_done, NORM_N[(r, s)])
                        elif kind == "ctx_mask":
                            u = step[1]
                            dve.wait_ge(res_done, NORM_N[(0, u // 2)])
                            link(nc.vector.tensor_reduce(largest[:], res[:, u, :], X_AXIS, ALU.max,
                                                         apply_absolute_value=True))
                            nc.vector.tensor_scalar(tok_mask[:, 1, u:u + 1], largest[:], 0.0, None, ALU.is_gt)\
                                .then_inc(tok_masked, 1)
                            dve.wait_ge(tok_masked, u + 1)
                        elif kind == "ctx_norm":
                            for u in range(NU):
                                statistics(c_tok, u, ctx_stats if u == NU - 1 else None, NU)
                            refine(slice(NU, 2 * NU), CTX_NORM["eps"], RSTD_N[step])
                            for u in range(NU):
                                i = nc.vector.tensor_scalar(c_work[:, u, :], c_tok[:, u, :], stat[:, NU + u, 0:1],
                                                            newton[:, NU + u:NU + u + 1], ALU.subtract, ALU.mult)
                            i.then_inc(ctx_normed, 1)
                            dve.wait_ge(ctx_normed, 1)
                        elif kind == "pick":
                            u = step[1]
                            bank = ring.wait_filled(dve, ("route", u))
                            nc.vector.tensor_tensor(logits[:, u, :], bank[:, 0:NE], ROW("router_b"), ALU.add)\
                                .then_inc(ring.read(("route", u)), 1)
                            ring.wait_read(dve, ("route", u))
                            link(nc.vector.max(best[:, u, :], logits[:, u, :]))
                            link(nc.vector.max_index(best_i[:, u, :], best[:, u, :], logits[:, u, :]))
                            nc.vector.tensor_tensor(share[:, u, 0:1], best[:, u, 1:2], best[:, u, 0:1],
                                                    ALU.subtract).then_inc(picked, 1)
                        elif kind == "gates":
                            s = step[1]
                            units = slice(2 * s, 2 * s + 2)
                            dve.wait_ge(gate_exp_done, GATES_N[s])
                            link(nc.vector.tensor_scalar(share[:, units, 2], share[:, units, 1], 1.0, None, ALU.add))
                            link(nc.vector.reciprocal(share[:, units, 2], share[:, units, 2]))
                            link(nc.vector.tensor_tensor(share[:, units, 3], share[:, units, 1], share[:, units, 2],
                                                         ALU.mult))
                            link(nc.vector.tensor_copy(best_f[:, units, :], best_i[:, units, 0:2]))
                            for u in (2 * s, 2 * s + 1):
                                for k in range(2):
                                    i = nc.vector.tensor_scalar(one_hot[:, k, u, :], K("iota", 0, NE),
                                                                best_f[:, u, k:k + 1], share[:, u, 2 + k:3 + k],
                                                                ALU.is_equal, ALU.mult)
                            link(i)
                            nc.vector.tensor_tensor(gates[:, units, :], one_hot[:, 0, units, :],
                                                    one_hot[:, 1, units, :], ALU.add).then_inc(gates_done, 1)
                            dve.wait_ge(gates_done, GATES_N[s])
                        elif kind == "add_bias":
                            u = step[1]
                            job = ("gate_bias", u)
                            bank = ring.wait_filled(dve, job)
                            nc.vector.tensor_tensor(raw[:, u, :], bank[:, 0:D], raw[:, u, :], ALU.add)\
                                .then_inc(ring.read(job), 1)
                            ring.wait_read(dve, job)
                        elif kind == "expert_down":
                            e, s = step[1:]
                            for j in range(2):
                                u = 2 * s + j
                                job = step + (j,)
                                bank = ring.wait_filled(dve, job)
                                nc.vector.scalar_tensor_tensor(raw[:, u, :], bank[:, 0:D], gates[:, u, e:e + 1],
                                                               raw[:, u, :], ALU.mult, ALU.add)\
                                    .then_inc(ring.read(job), 1)
                                ring.wait_read(dve, job)

                @block.gpsimd
                def _(pool):
                    steps_done = [0]

                    def link(i):
                        steps_done[0] += 1
                        i.then_inc(pool_step, 1)
                        pool.wait_ge(pool_step, steps_done[0])

                    for step in steps:
                        kind = step[0]
                        if kind == "lengths":
                            a, s = step[1:]
                            pool.wait_ge(counted, LEN_N[(a, s)])
                            nc.gpsimd.tensor_tensor(
                                len_mask[:, s, :].rearrange("p (h k) -> p h k", k=T),
                                K("own_head").rearrange("p (h o) -> p h o", o=1).to_broadcast([P, H, T]),
                                late[:].rearrange("p (o k) -> p o k", o=1).to_broadcast([P, H, T]), ALU.mult)\
                                .then_inc(len_masked, 1)
                        elif kind == "norm":
                            r, s = step[1:]
                            norm = NORMS[r]
                            units = slice(2 * s, 2 * s + 2)

                            def by(name):
                                return ROW(name).rearrange("p (o d) -> p o d", o=1).to_broadcast([P, 2, D])

                            src = res if r == LN_ONLY else raw
                            pool.wait_ge(normed_done, NORM_N[(r, s)])
                            if norm["post"]:
                                link(nc.gpsimd.tensor_tensor(res[:, units, :], normed[:, units, :], by(f"g{r}"), ALU.mult))
                                i = nc.gpsimd.tensor_tensor(res[:, units, :], res[:, units, :], by(f"b{r}"), ALU.add)
                                if norm["add"]:
                                    link(i)
                                    i = nc.gpsimd.tensor_tensor(res[:, units, :], res[:, units, :], by(f"add{r}"), ALU.add)
                            elif norm["add"]:
                                i = nc.gpsimd.tensor_tensor(res[:, units, :], src[:, units, :], by(f"add{r}"), ALU.add)
                            if norm["post"] or norm["add"]:
                                i.then_inc(res_done, 1)
                        elif kind == "ctx_mask":
                            u = step[1]
                            pool.wait_ge(tok_masked, u + 1)
                            nc.gpsimd.tensor_scalar(c_work[:, u, :], c_tok[:, u, :], tok_mask[:, 1, u:u + 1], None,
                                                    ALU.mult).then_inc(ctx_masked, 1)
                        elif kind in ("q", "k") and SITES[step[1]]["rope"]:
                            a, s = step[1:]
                            k, dst = (0, qT) if kind == "q" else (1, kT)
                            ring.wait_read(pool, step + (kind,))
                            ring.wait_read(pool, step + (kind + "p",))
                            nc.gpsimd.tensor_tensor(dst[:, s * SW:(s + 1) * SW], rope_a[:, k, :], rope_b[:, k, :],
                                                    ALU.add).then_inc(rope_done, 1)

                @block.sync
                def _(sp):
                    ring.wait_filled(sp, ("ctx_turn", 3, NS - 1))
                    sp.wait_ge(ctx_normed, 1)
                    sp.dma_start(c_tok[:], token_major(ctx[tile])).then_inc(next_in, 16)
                    sp.wait_ge(masks_read, 1)
                    load_masks(sp, tile, next_in)
                    sp.wait_ge(stats_done, NORM_N[(AFTER_SITE[7], NS - 1)])
                    sp.dma_start(res[:], token_major(x[tile])).then_inc(next_in, 16)
                    for u in range(NU):
                        ring.wait_read(sp, ("expert_down", NE - 1, u // 2, u % 2))
                    sp.dma_start(token_major(out[tile]), raw[:]).then_inc(raw_free, 16)
                    sp.wait_ge(next_in, 16 * (2 + 2))

            with nc.Block() as block:
                @block.sync
                def _(sp):
                    for s in per_tile:
                        sp.sem_clear(s)

        with nc.Block() as block:
            @block.sync
            def _(sp):
                sp.wait_ge(raw_free, 16 * ITERS + 16)


def _halves(w, heads, dk):
    w = w.reshape(w.shape[0], heads, dk)
    return np.concatenate([w[:, 0::2].reshape(w.shape[0], -1), w[:, 1::2].reshape(w.shape[0], -1)], axis=1)


def _rotated(w):
    w = w.reshape(w.shape[0], H, 2, DK // 2)
    return w[:, :, ::-1].reshape(w.shape[0], -1)


def _by_rows(w):
    n = w.shape[0] // P
    return w.reshape(n, P, w.shape[1]).transpose(1, 0, 2).reshape(P, -1)


def lay_out(t):
    wq, cols, rows = {}, {}, {}
    for r, norm in enumerate(NORMS):
        cols[f"g{r}"], cols[f"b{r}"] = t[norm["g"]][:, None], t[norm["b"]][:, None]
        if norm["post"]:
            rows[f"g{r}"], rows[f"b{r}"] = t[norm["g"]], t[norm["b"]]
        if norm["add"]:
            rows[f"add{r}"] = t[norm["add"]]
    cols["gc"], cols["bc"] = t[CTX_NORM["g"]][:, None], t[CTX_NORM["b"]][:, None]
    for a, site in enumerate(SITES):
        layer = site["layer"]
        if layer == 0:
            n = 2 if site["cross"] else 1
            w = {k: t[f"L0_xattn_W{k}{n}"].transpose(1, 0, 2).reshape(D, D) for k in "qkv"}
            b = {}
        elif layer in (1, 2):
            pre = f"L{layer}_xattn_{'ca' if site['cross'] else 'sa'}_"
            w = {k: t[f"{pre}w{k}"] for k in "qkvo"}
            b = {k: t[f"{pre}b{k}"] for k in "qkv"}
        else:
            pre = f"L3_xattn_{'ca' if site['cross'] else 'sa'}_"
            w = {k: t[pre + "in_w"][n * D:(n + 1) * D].T for n, k in enumerate("qkv")}
            w["o"] = t[pre + "out_w"].T
            b = {k: t[pre + "in_b"][n * D:(n + 1) * D] for n, k in enumerate("qkv")}
        dk = DKB if site["wide"] else DK
        wq[f"wq{a}"], wq[f"wk{a}"] = w["q"], w["k"]
        wq[f"wv{a}"] = _halves(w["v"], H, dk)
        if site["rope"]:
            wq[f"wqp{a}"], wq[f"wkp{a}"] = _rotated(w["q"]), _rotated(w["k"])
            cols[f"bqp{a}"], cols[f"bkp{a}"] = _rotated(b["q"][None]).T, _rotated(b["k"][None]).T
        if site["out"]:
            wq[f"wo{a}"] = _by_rows(w["o"])
        if site["bias"]:
            cols[f"bq{a}"], cols[f"bk{a}"] = b["q"].reshape(-1, P).T, b["k"].reshape(-1, P).T
            rows[f"bv{a}"] = _halves(b["v"][None], H, dk)[0]
    up = {0: t["L0_xattn_fc1_w"].T, 1: t["L1_xattn_ffn_w1"], 2: t["L2_xattn_fc1_w"]}
    down = {0: t["L0_xattn_fc2_w"].T, 1: t["L1_xattn_ffn_w2"], 2: t["L2_xattn_fc2_w"]}
    up_b = {0: t["L0_xattn_fc1_b"], 1: t["L1_xattn_ffn_b1"], 2: t["L2_xattn_fc1_b"]}
    for n in FFN_WIDTH:
        wq[f"up{n}"], wq[f"down{n}"] = up[n], _by_rows(down[n])
        cols[f"up_b{n}"] = up_b[n].reshape(-1, P).T
    wq["router"] = t["L3_xattn_router_w"].T
    for e in range(NE):
        wq[f"up_e{e}"] = t["L3_xattn_e_fc1_w"][e].T
        wq[f"down_e{e}"] = _by_rows(t["L3_xattn_e_fc2_w"][e].T)
        cols[f"up_be{e}"] = t["L3_xattn_e_fc1_b"][e].reshape(-1, P).T
    rows["down_b0"] = t["L0_xattn_fc2_b"]
    rows["router_b"] = t["L3_xattn_router_b"]
    weights = np.concatenate([wq[k] for k in W_AT], axis=1)
    columns = np.concatenate([cols[k] for k in C_AT], axis=1)
    row = np.concatenate([rows[k] for k in R_AT])[None]
    return weights, columns, row


def shape_constants():
    c = {}
    part = np.arange(P)
    c["ident"] = np.eye(P)
    c["head_of_four"] = (part[:, None] // DK % 4 == np.arange(4)[None]).astype(np.float32)
    c["causal"] = np.where(np.arange(T)[None] > (part % T)[:, None], -4 * BIG, 0.0)
    c["iota"] = np.broadcast_to(np.arange(T), (P, T))
    c["head_of_all"] = (part[:, None] // DK == np.arange(32)[None]).astype(np.float32)
    c["own_head"] = (part[:, None] % 32 == np.arange(H)[None]).astype(np.float32)
    c["own_rows"] = (part[:, None] // 32 == np.arange(SB)[None]).astype(np.float32)
    c["eps_small"], c["eps_large"] = np.full((P, 1), EPS_SMALL), np.full((P, 1), EPS_LARGE)
    inv = (1.0 / np.float32(10000.0) ** (np.arange(0, DK, 2, dtype=np.float32) / np.float32(DK))).astype(np.float32)
    angle = np.outer(np.arange(T, dtype=np.float32), inv).astype(np.float32)
    cos, sin = np.cos(angle), np.sin(angle)
    d = part % DK
    sign = np.where(d < DK // 2, -1.0, 1.0)[:, None]
    c["cos"] = np.tile(cos.T[d % (DK // 2)], (1, SW // T))
    c["sin"] = np.tile(sin.T[d % (DK // 2)] * sign, (1, SW // T))
    return np.ascontiguousarray(np.concatenate([c[k] for k in K_AT], axis=1).astype(np.float32))


def kernel(**inputs):
    import concourse.bacc as bacc
    from concourse.bass_utils import run_bass_kernel_spmd

    t = {k: np.asarray(v) for k, v in inputs.items()}
    weights, columns, rows = lay_out(t)
    def turned(a):
        return np.roll(a, -1, axis=0)

    arrays = {
        "x": turned(t["x"].reshape(ITERS, NU, P, D)),
        "ctx": turned(t["ctx_1024"].reshape(ITERS, NU, P, D)),
        "mask": turned(t["mask_BxS2_bf1"].view(np.uint8).reshape(ITERS, NB, T)),
        "weights": weights,
        "columns": columns,
        "rows": rows,
        "constants": shape_constants(),
        "expert_bias": t["L3_xattn_e_fc2_b"],
    }
    arrays = {k: np.ascontiguousarray(v) for k, v in arrays.items()}
    nc = bacc.Bacc("TRN2", target_bir_lowering=False, num_devices=1)
    args = [nc.dram_tensor(k, a.shape, mybir.dt.from_np(a.dtype), kind="ExternalInput").ap() for k, a in arrays.items()]
    out = nc.dram_tensor("out", (ITERS, NU, P, D), F32, kind="ExternalOutput").ap()
    decoder_stack(nc, *args, out)
    r = run_bass_kernel_spmd(nc, [arrays], core_ids=[0])
    return r.results[0]["out"].reshape(B, T, D)
```
